# Optimizing a Trainium2 kernel written in Bass

```python
import numpy as np
import jax
import jax.numpy as jnp

def _softmax(x, axis=-1):
    return jax.nn.softmax(x, axis=axis)

def _gelu(x):
    return jax.nn.gelu(x, approximate=True)

def _silu(x):
    return jax.nn.silu(x)

def _sigmoid(x):
    return jax.nn.sigmoid(x)

def _layernorm(x, axis=-1, eps=1e-05):
    m = jnp.mean(x, axis=axis, keepdims=True)
    v = jnp.var(x, axis=axis, keepdims=True)
    return (x - m) / jnp.sqrt(v + eps)

def _scatter_add(tgt, idx, src, axis=0):
    return tgt.at[idx].add(src)

def _segment_sum(src, seg, n):
    return jax.ops.segment_sum(src, seg, n)
kernel_name = 'mk_xattn_seq_d2_seqx_r2_ea539b'

def setup_inputs(seed: int=0):
    np.random.seed(seed)
    _w = jnp.asarray

    def _rec_inputs():
        import jax
        import jax.numpy as jnp
        _rk = jax.random.key(seed)
        x = -0.0002928 + 1 * jax.random.normal(jax.random.fold_in(_rk, 1), (4, 1024, 512), jnp.float32)
        _lenS = 1024 - jax.random.randint(jax.random.fold_in(_rk, 7), (4,), 0, max(1, 1024 // 4) + 1, jnp.int32)
        _lenS2 = 1024 - jax.random.randint(jax.random.fold_in(_rk, 8), (4,), 0, max(1, 1024 // 4) + 1, jnp.int32)
        _ctx_768P = jax.random.normal(jax.random.fold_in(_rk, 11), (4, 16, 384), jnp.float32)
        _ctx_768c = jax.random.dirichlet(jax.random.fold_in(_rk, 511), 0.3 * jnp.ones((16,), jnp.float32), (4, 1024))
        _ctx_768t = jnp.einsum('bsk,bkd->bsd', _ctx_768c, _ctx_768P)
        _ctx_768t = _ctx_768t * jax.lax.rsqrt(jnp.mean(jnp.square(_ctx_768t)) + 1e-12) * 0.953939
        ctx_768 = 2.09791e-05 + 1.00001 * (_ctx_768t + 0.3 * jax.random.normal(jax.random.fold_in(_rk, 611), (4, 1024, 384), jnp.float32))
        return (x, ctx_768)
    x, ctx_768 = _rec_inputs()

    def _L0_xattn_setup():
        import jax, jax.numpy as jnp
        import numpy as np
        D_Q, D_CTX, N_HEADS, HEAD_DIM = (512, 384, 16, 64)
        INNER = N_HEADS * HEAD_DIM
        EPS = 1e-05

        def _layernorm(x, gamma, beta):
            mu = jnp.mean(x, axis=-1, keepdims=True)
            var = jnp.var(x, axis=-1, keepdims=True)
            return (x - mu) * jax.lax.rsqrt(var + EPS) * gamma + beta
        key = jax.random.key(seed)
        ks = jax.random.split(key, 8)
        B, NQ, NC = (4, 512, 512)
        s_q = 1.0 / np.sqrt(D_Q)
        s_c = 1.0 / np.sqrt(D_CTX)
        s_i = 1.0 / np.sqrt(INNER)
        return {'x': jax.random.normal(ks[0], (B, NQ, D_Q), jnp.float32), 'context': jax.random.normal(ks[1], (B, NC, D_CTX), jnp.float32), 'Wq': jax.random.normal(ks[2], (D_Q, INNER), jnp.float32) * s_q, 'Wk': jax.random.normal(ks[3], (D_CTX, INNER), jnp.float32) * s_c, 'Wv': jax.random.normal(ks[4], (D_CTX, INNER), jnp.float32) * s_c, 'Wo': jax.random.normal(ks[5], (INNER, D_Q), jnp.float32) * s_i, 'bo': jnp.zeros((D_Q,), jnp.float32), 'gamma': jnp.ones((D_Q,), jnp.float32), 'beta': jnp.zeros((D_Q,), jnp.float32)}
    _L0_xattn_all = _L0_xattn_setup()
    _L0_xattn_in = {k: v for k, v in _L0_xattn_all.items() if k in ('Wq', 'Wk', 'Wv', 'Wo', 'bo', 'gamma', 'beta')}
    del _L0_xattn_all

    def _L1_xattn_setup():
        import jax, jax.numpy as jnp
        import numpy as np
        EPS_RMS = 1e-05
        EPS_L2 = 1e-12
        MAX_SEQ_LEN = 2048
        D_Q, D_KV, N_HEADS = (512, 384, 16)
        HEAD_DIM = D_Q // N_HEADS

        def _rope_tables(head_dim, max_len):
            inv_freq = 1.0 / 10000.0 ** (np.arange(0, head_dim, 2, dtype=np.float32) / head_dim)
            t = np.arange(max_len, dtype=np.float32)
            freqs = np.einsum('i,j->ij', t, inv_freq)
            emb = np.concatenate([freqs, freqs], axis=-1)
            return (jnp.asarray(np.cos(emb)), jnp.asarray(np.sin(emb)))

        def _rotate(x, cos, sin):
            T = x.shape[1]
            c = cos[:T][None, :, None, :]
            s = sin[:T][None, :, None, :]
            x1, x2 = jnp.split(x, 2, axis=-1)
            return x * c + jnp.concatenate([-x2, x1], axis=-1) * s
        key = jax.random.key(seed)
        ks = jax.random.split(key, 6)
        B, T_dec, T_enc = (4, 256, 1024)
        x = jax.random.normal(ks[0], (B, T_dec, D_Q), dtype=jnp.float32)
        encoder_out = jax.random.normal(ks[1], (B, T_enc, D_KV), dtype=jnp.float32)
        sq = 1.0 / np.sqrt(D_Q)
        skv = 1.0 / np.sqrt(D_KV)
        norm_w = jnp.ones((D_Q,), dtype=jnp.float32)
        wq = jax.random.normal(ks[2], (D_Q, D_Q), dtype=jnp.float32) * sq
        wkv = jax.random.normal(ks[3], (D_KV, 2 * D_Q), dtype=jnp.float32) * skv
        wout = jax.random.normal(ks[4], (D_Q, D_Q), dtype=jnp.float32) * sq
        return {'x': x, 'encoder_out': encoder_out, 'norm_w': norm_w, 'wq': wq, 'wkv': wkv, 'wout': wout}
    _L1_xattn_all = _L1_xattn_setup()
    _L1_xattn_in = {k: v for k, v in _L1_xattn_all.items() if k in ('norm_w', 'wq', 'wkv', 'wout')}
    del _L1_xattn_all
    return {'x': x, 'ctx_768': ctx_768, 'L0_xattn_Wq': _L0_xattn_in['Wq'], 'L0_xattn_Wk': _L0_xattn_in['Wk'], 'L0_xattn_Wv': _L0_xattn_in['Wv'], 'L0_xattn_Wo': _L0_xattn_in['Wo'], 'L0_xattn_bo': _L0_xattn_in['bo'], 'L0_xattn_gamma': _L0_xattn_in['gamma'], 'L0_xattn_beta': _L0_xattn_in['beta'], 'L1_xattn_norm_w': _L1_xattn_in['norm_w'], 'L1_xattn_wq': _L1_xattn_in['wq'], 'L1_xattn_wkv': _L1_xattn_in['wkv'], 'L1_xattn_wout': _L1_xattn_in['wout']}

def reference(x, ctx_768, L0_xattn_Wq, L0_xattn_Wk, L0_xattn_Wv, L0_xattn_Wo, L0_xattn_bo, L0_xattn_gamma, L0_xattn_beta, L1_xattn_norm_w, L1_xattn_wq, L1_xattn_wkv, L1_xattn_wout):
    import jax
    import jax.numpy as jnp

    def _L0_xattn_ref(x, context, Wq, Wk, Wv, Wo, bo, gamma, beta):
        import jax, jax.numpy as jnp
        import numpy as np
        D_Q, D_CTX, N_HEADS, HEAD_DIM = (512, 384, 16, 64)
        INNER = N_HEADS * HEAD_DIM
        EPS = 1e-05

        def _layernorm(x, gamma, beta):
            mu = jnp.mean(x, axis=-1, keepdims=True)
            var = jnp.var(x, axis=-1, keepdims=True)
            return (x - mu) * jax.lax.rsqrt(var + EPS) * gamma + beta
        scale = HEAD_DIM ** (-0.5)
        h = _layernorm(x, gamma, beta)
        B, NQ, _ = x.shape
        NC = context.shape[1]
        Q = (h @ Wq).reshape(B, NQ, N_HEADS, HEAD_DIM)
        K = (context @ Wk).reshape(B, NC, N_HEADS, HEAD_DIM)
        V = (context @ Wv).reshape(B, NC, N_HEADS, HEAD_DIM)
        attn = jnp.einsum('bihd,bjhd->bhij', Q, K)
        attn = jax.nn.softmax(attn, axis=-1) * scale
        vals = jnp.einsum('bhij,bjhd->bihd', attn, V).reshape(B, NQ, INNER)
        out = vals @ Wo + bo
        return x + out

    def _L1_xattn_ref(x, encoder_out, norm_w, wq, wkv, wout):
        import jax, jax.numpy as jnp
        import numpy as np
        EPS_RMS = 1e-05
        EPS_L2 = 1e-12
        MAX_SEQ_LEN = 2048
        D_Q, D_KV, N_HEADS = (512, 384, 16)
        HEAD_DIM = D_Q // N_HEADS

        def _rope_tables(head_dim, max_len):
            inv_freq = 1.0 / 10000.0 ** (np.arange(0, head_dim, 2, dtype=np.float32) / head_dim)
            t = np.arange(max_len, dtype=np.float32)
            freqs = np.einsum('i,j->ij', t, inv_freq)
            emb = np.concatenate([freqs, freqs], axis=-1)
            return (jnp.asarray(np.cos(emb)), jnp.asarray(np.sin(emb)))

        def _rotate(x, cos, sin):
            T = x.shape[1]
            c = cos[:T][None, :, None, :]
            s = sin[:T][None, :, None, :]
            x1, x2 = jnp.split(x, 2, axis=-1)
            return x * c + jnp.concatenate([-x2, x1], axis=-1) * s
        B, T_dec, _ = x.shape
        T_enc = encoder_out.shape[1]
        cos, sin = _rope_tables(HEAD_DIM, MAX_SEQ_LEN)
        residual = x
        xn = x * jax.lax.rsqrt(jnp.mean(x * x, axis=-1, keepdims=True) + EPS_RMS) * norm_w
        q = (xn @ wq).reshape(B, T_dec, N_HEADS, HEAD_DIM)
        kv = (encoder_out @ wkv).reshape(B, T_enc, 2, N_HEADS, HEAD_DIM)
        k, v = (kv[:, :, 0], kv[:, :, 1])
        q = _rotate(q, cos, sin)
        k = _rotate(k, cos, sin)
        q = q / jnp.maximum(jnp.linalg.norm(q, axis=-1, keepdims=True), EPS_L2)
        k = k / jnp.maximum(jnp.linalg.norm(k, axis=-1, keepdims=True), EPS_L2)
        scale = jnp.sqrt(jnp.float32(HEAD_DIM))
        logits = jnp.einsum('bqhd,bkhd->bhqk', q, k) * scale
        attn = jax.nn.softmax(logits, axis=-1)
        out = jnp.einsum('bhqk,bkhd->bqhd', attn, v).reshape(B, T_dec, D_Q)
        return residual + out @ wout
    x = _L0_xattn_ref(x, ctx_768, L0_xattn_Wq, L0_xattn_Wk, L0_xattn_Wv, L0_xattn_Wo, L0_xattn_bo, L0_xattn_gamma, L0_xattn_beta)
    x = _L1_xattn_ref(x, ctx_768, L1_xattn_norm_w, L1_xattn_wq, L1_xattn_wkv, L1_xattn_wout)
    return x

_drawn_inputs = setup_inputs


def setup_inputs(seed=0):
    import zlib

    import numpy as np

    out = dict(_drawn_inputs(seed))
    spreads = {'L0_xattn_bo': (0.0, 0.1),
     'L0_xattn_gamma': (1.0, 0.2),
     'L0_xattn_beta': (0.0, 0.313),
     'L1_xattn_norm_w': (1.0, 0.6)}
    factors = {}
    for name, (base, spread) in spreads.items():
        noise = np.random.default_rng([zlib.crc32(name.encode()), seed]).standard_normal(out[name].shape)
        drawn = base * np.exp(spread * noise) if base else spread * noise
        out[name] = jnp.asarray(drawn.astype(out[name].dtype))
    for name, factor in factors.items():
        out[name] = (out[name] * factor).astype(out[name].dtype)
    return out
```

```python
from contextlib import ExitStack

import numpy as np

import concourse.bass as bass
from concourse import mybir

F32 = mybir.dt.float32
F32R = mybir.dt.float32r
F16 = mybir.dt.float16
ALU = mybir.AluOpType
ACT = mybir.ActivationFunctionType
AX = mybir.AxisListType

B, S, D, DC = 4, 1024, 512, 384
P = 128
TT = S // P
NH = S // 512
XC, CC = D // P, DC // P
HEADS = 16
D0, D1 = 64, D // HEADS
G0, G1 = P // D0, P // D1
TURNS0, TURNS1 = HEADS // G0, HEADS // G1
KT = S // P
LN_EPS = RMS_EPS = 1e-5
L2_EPS = 1e-12
QK_SCALE = 64.0
PRIMED = 1
RING = 8


def _x(a, b):
    return [("rowmax", i) for i in range(a, b)]


SIDE0 = [[("k", 0), ("k", 1)], [("q", 0), ("q", 1)], _x(0, 5), _x(5, 11), _x(11, 17),
         _x(17, 23) + [("shift", 0), ("shift", 1)], _x(23, 29) + [("v", 0)],
         _x(29, 32) + [("v", 1), ("shift", 2), ("shift", 3)]]
SIDE1 = [[("k", 0), ("k", 1)], [("q", 0), ("q", 1)], [("v", 0), ("v", 1)], [], [], [],
         [("turn_k", h) for h in range(G1)], [("turn_q", h) for h in range(G1)]]
POST = [[("den", 0), ("den", 1)], [], [("out", 0), ("out", 1)], [("out", 2), ("out", 3)],
        [("out", 4), ("out", 5)], [("out", 6), ("out", 7)], [], []]


def chunk(layer, kt, side, post):
    return (POST[kt] if post else []) + ((SIDE0, SIDE1)[layer][kt] if side else [])


def n_units(layer, side, post):
    return sum(len(chunk(layer, kt, side, post)) for kt in range(KT))


PREP_UNITS = (CC + XC) * NH
MID_UNITS = XC * NH
TURNS = (TURNS0, TURNS1)
STEPS = (KT * G0, KT * G1)
ADDS = ((KT - 1) * G0, (KT - 1) * G1)
BODY = tuple(n_units(l, True, True) for l in (0, 1))
FIRST = tuple(n_units(l, True, False) for l in (0, 1))
LAST = n_units(0, False, True)


def layer_units(l):
    return 2 * FIRST[l] + (TURNS[l] - 2) * BODY[l] + 2 * LAST


BATCH_UNITS = PREP_UNITS + layer_units(0) + MID_UNITS + layer_units(1)
TURNS_B = sum(TURNS)


def side0_start(b, l):
    return b * (BATCH_UNITS // 2) + (PREP_UNITS + l * (layer_units(0) + MID_UNITS)) // 2


class Counts:

    def __init__(self, b, l, p):
        self.bank = side0_start(b, l) + FIRST[l] // 2
        if not (isinstance(p, int) and p == 0):
            self.bank = self.bank + FIRST[l] // 2 + (p - 1) * (BODY[l] // 2)
        self.turns = b * TURNS_B + l * TURNS0 + p
        self.avs = self.turns * KT
        self.steps = (b * (TURNS0 * STEPS[0] + TURNS1 * STEPS[1]) + l * TURNS0 * STEPS[0]
                      + p * STEPS[l])
        self.adds = (b * (TURNS0 * ADDS[0] + TURNS1 * ADDS[1]) + l * TURNS0 * ADDS[0]
                     + p * ADDS[l])
        self.sides = b * TURNS[l] + p


class Share:

    def __init__(self, b, layer, par, turns, adds, sides, w_count):
        self.b, self.layer, self.par = b, layer, par
        self.turns, self.adds, self.sides, self.w_count = turns, adds, sides, w_count


def build(nc, x, ctx_in, wq0, wk0, wv0, wo0, bo, gamma, beta, norm_w, wq1, wkv1, wout1,
          cos_t, sin_t, ident_t, out):
    W0 = {"q": wq0.rearrange("(c p) n -> p c n", p=P), "k": wk0.rearrange("(c p) n -> p c n", p=P),
          "v": wv0.rearrange("(c p) n -> p c n", p=P), "o": wo0}
    kv1 = wkv1.rearrange("(c p) n -> p c n", p=P)
    W1 = {"q": wq1.rearrange("(c p) n -> p c n", p=P), "k": kv1[:, :, 0:D], "v": kv1[:, :, D:2 * D],
          "o": wout1}
    WEIGHTS = (W0, W1)
    x_rows = x.rearrange("b (t p) d -> b p t d", p=P)
    c_rows = ctx_in.rearrange("b (t p) d -> b p t d", p=P)
    out_rows = out.rearrange("b (t p) d -> b p t d", p=P)

    with ExitStack() as ctx:
        def sb(name, shape, dt=F32, scope=ctx):
            return scope.enter_context(nc.sbuf_tensor(name, shape, dt))

        def sem(name):
            return ctx.enter_context(nc.semaphore(name))

        ident = sb("ident", [P, P])
        ident_r = sb("ident_r", [P, P], F32R)
        ident_h = sb("ident_h", [P, P], F16)
        ones = [sb("ones_scaled", [P, D0]), sb("ones_plain", [P, D0])]
        cos = sb("cos", [P, TT, D1])
        sin = sb("sin", [P, TT, D1])
        affine = sb("affine", [P, 3, XC])
        bo_all = sb("bo_all", [P, D])
        stats = sb("stats", [P, TT, 6])
        mv = sb("mv", [P, TT, 2])
        var_eps = sb("var_eps", [P, TT])
        mean_sq = sb("mean_sq", [P, TT])
        rstd = sb("rstd", [P, TT])
        gate_v = sb("gate_v", [P, 6])
        gate_p = sb("gate_p", [P, 10])
        power = sb("power", [P, TT * G1])
        resid = sb("resid", [P, TT, D])
        hT = sb("hT", [P, XC, S])
        cT = sb("cT", [P, CC, S])
        wq = [sb(f"wq{i}", [P, XC, P]) for i in range(2)]
        wk = [sb(f"wk{i}", [P, CC, P]) for i in range(2)]
        wv = [sb(f"wv{i}", [P, CC, P]) for i in range(2)]
        wo = [sb(f"wo{i}", [P, D]) for i in range(2)]
        v_tok = [sb(f"v_tok{i}", [P, KT, P]) for i in range(2)]
        probs = sb("probs", [P, RING, S])
        acc = [sb(f"acc{h}", [P, S]) for h in range(G1)]
        o_raw = sb("o_raw", [P, S])
        recip = sb("recip", [P, S])
        o_norm = sb("o_norm", [P, S])
        xn = probs[:, 0:4, :].rearrange("p a b -> p (a b)").rearrange("p (t d) -> p t d", d=D)
        c_raw = probs[:, 4:7, :].rearrange("p a b -> p (a b)").rearrange("p (t d) -> p t d", d=DC)

        with ExitStack() as scope:
            k_parts = [[sb(f"k_parts{i}{h}", [P, S], F32R, scope) for h in range(G0)] for i in range(2)]
            k_one = [[sb(f"k_one{i}{h}", [D0 + 1, S], F32R, scope) for h in range(G0)] for i in range(2)]
            q_high = [[sb(f"q_high{i}{h}", [P, S], F32R, scope) for h in range(G0)] for i in range(2)]
            q_low = [[sb(f"q_low{i}{h}", [D0 + 1, S], F32R, scope) for h in range(G0)] for i in range(2)]
            tile_max = sb("tile_max", [P, G0, TT, NH], F32, scope)
            neg_max = sb("neg_max", [P, G0, TT], F32R, scope)
        with ExitStack() as scope:
            kT = [sb(f"kT{i}", [P, G1, S], F16, scope) for i in range(2)]
            qT = [sb(f"qT{i}", [P, G1, S], F16, scope) for i in range(2)]
            stack = [sb(f"stack{n}", [P, TT * G1, 4, D1], F16, scope) for n in ("k", "q")]
            raw = [sb(f"raw{n}", [P, TT, G1, D1], F32, scope) for n in ("k", "q")]
            rot = sb("rot", [P, TT, G1, D1], F32, scope)
            tmp = sb("tmp", [P, TT, G1, D1], F32, scope)
            sumsq = sb("sumsq", [P, TT * G1], F32, scope)
            inv = sb("inv", [P, TT * G1], F32, scope)

        scores = [ctx.enter_context(nc.psum_tensor(f"scores{i}", [P, S], F32)) for i in range(2)]
        o_acc = ctx.enter_context(nc.psum_tensor("o_acc", [P, S], F32))
        work = [ctx.enter_context(nc.psum_tensor(f"work{i}", [P, 512], F32)) for i in range(2)]
        work_h = [w[:, :].bitcast(F16) for w in work]

        consts_in = sem("consts_in")
        consts_ok = sem("consts_ok")
        x_in = sem("x_in")
        c_in = sem("c_in")
        w_in = [sem(f"w_in{i}") for i in range(2)]
        wo_in = [sem(f"wo_in{i}") for i in range(2)]
        stored = sem("stored")
        bn_ok = sem("bn_ok")
        aggr_ok = sem("aggr_ok")
        mean_sq_step = sem("mean_sq_step")
        var_ok = sem("var_ok")
        rstd_ok = sem("rstd_ok")
        xn_ok = sem("xn_ok")
        bias_ok = sem("bias_ok")
        power_ok = sem("power_ok")
        work_full = sem("work_full")
        work_free = [sem(f"work_free{i}") for i in range(2)]
        high_ok = sem("high_ok")
        dup_ok = sem("dup_ok")
        neg_max_ok = sem("neg_max_ok")
        scores_ok = sem("scores_ok")
        exp_ok = sem("exp_ok")
        add_ok = sem("add_ok")
        av_ok = sem("av_ok")
        o_copied = sem("o_copied")
        o_norm_ok = sem("o_norm_ok")
        rope_step = sem("rope_step")
        norm_step = sem("norm_step")
        ROPE_STEPS, NORM_STEPS = 10, 3
        def sides_of(b, l, p, par, j=None):
            t = Counts(b, l, p)
            half_side, half_post = (j + 1, j) if j is not None else ((p + 1) // 2, (p - 1) // 2)
            loads = b * (TURNS_B // 2) + l * (TURNS0 // 2)
            side = Share(b, l, 1 - par, None, None, t.sides + 1, 16 * 3 * (loads + half_side + 1))
            post = Share(b, l, 1 - par, t.turns, t.adds, None, 16 * (loads + half_post + 1))
            return side, post

        def run_layer(eng, b, l, unit, one_turn, extra=None):
            side, _ = sides_of(b, l, -1, 1)
            u = 0
            for kt in range(KT):
                for kind, i in chunk(l, kt, True, False):
                    unit(kind, i, side0_start(b, l), u, side, None)
                    u += 1
                if extra is not None and l == 1:
                    extra(kt, side, side0_start(b, 1), False)
            one_turn(l, b, 0, 0, True, False)
            if l == 0:
                with eng.Fori(0, (TURNS0 - 2) // 2) as j:
                    for i in range(2):
                        one_turn(l, b, 2 * j + 1 + i, 1 - i, False, False, j)
            else:
                for p in range(1, TURNS1 - 1):
                    one_turn(l, b, p, p % 2, False, False)
            p = TURNS[l] - 1
            one_turn(l, b, p, p % 2, False, True)
            _, post = sides_of(b, l, p + 1, (p + 1) % 2)
            bank = Counts(b, l, p).bank + LAST // 2
            u = 0
            for kt in range(KT):
                for kind, i in chunk(l, kt, False, True):
                    unit(kind, i, bank, u, None, post)
                    u += 1

        block = ctx.enter_context(nc.Block())

        def wait_unit_evacuated(eng, bank, u):
            eng.wait_ge(work_free[u % 2], PRIMED + bank + (u // 2 + 1))

        def wait_all_evacuated(eng, bank):
            for i in range(2):
                eng.wait_ge(work_free[i], PRIMED + bank)

        def tokens(n):
            return slice(n * 512, (n + 1) * 512)

        def tile(t):
            return slice(t * P, (t + 1) * P)

        @block.sync
        def _(sp):
            for dst, src in ((ident[:, :], ident_t), (cos[:, :, :], cos_t.rearrange("(t p) d -> p t d", p=P)),
                             (sin[:, :, :], sin_t.rearrange("(t p) d -> p t d", p=P)),
                             (affine[:, 0, :], gamma.rearrange("(c p) -> p c", p=P)),
                             (affine[:, 1, :], beta.rearrange("(c p) -> p c", p=P)),
                             (affine[:, 2, :], norm_w.rearrange("(c p) -> p c", p=P)),
                             (bo_all[:, :], bo.rearrange("(a n) -> a n", a=1).to_broadcast([P, D]))):
                with nc.allow_non_contiguous_dma("small constants, once"):
                    sp.dma_start(dst, src).then_inc(consts_in, 16)

            def load_side(l, p, par):
                for name, dst in (("q", wq), ("k", wk), ("v", wv)):
                    sp.dma_start(dst[par][:, :, :], WEIGHTS[l][name][:, :, bass.ds(p * P, P)]).then_inc(w_in[par], 16)

            def load_out(l, p, par):
                sp.dma_start(wo[par][:, :], WEIGHTS[l]["o"][bass.ds(p * P, P), :]).then_inc(wo_in[par], 16)

            def after(b, l, p):
                sp.wait_ge(work_full, 2 * Counts(b, l, p).bank)

            load_side(0, 0, 0)
            load_side(0, 1, 1)
            with sp.Fori(0, B) as b:
                sp.wait_ge(stored, 16 * (PRIMED + b))
                sp.dma_start(c_raw, c_rows[bass.ds(b, 1), :, :, :].rearrange("a p t d -> p (a t) d")).then_inc(c_in, 16)
                sp.dma_start(resid[:, :, :], x_rows[bass.ds(b, 1), :, :, :].rearrange("a p t d -> p (a t) d")).then_inc(x_in, 16)
                after(b, 0, 0)
                load_out(0, 0, 0)
                load_side(0, 2, 0)
                with sp.Fori(0, (TURNS0 - 4) // 2) as j:
                    for i in range(2):
                        p = 2 * j + 1 + i
                        after(b, 0, p)
                        load_out(0, p, 1 - i)
                        load_side(0, p + 2, 1 - i)
                after(b, 0, TURNS0 - 3)
                load_out(0, TURNS0 - 3, 1)
                load_side(0, TURNS0 - 1, 1)
                for p in (TURNS0 - 2, TURNS0 - 1):
                    after(b, 0, p)
                    load_out(0, p, p % 2)
                    load_side(1, p - (TURNS0 - 2), p % 2)
                for p in range(TURNS1):
                    after(b, 1, p)
                    load_out(1, p, p % 2)
                    if p < TURNS1 - 2:
                        load_side(1, p + 2, p % 2)
                    else:
                        load_side(0, p - (TURNS1 - 2), p % 2)
                wait_all_evacuated(sp, (b + 1) * (BATCH_UNITS // 2))
                sp.dma_start(out_rows[bass.ds(b, 1), :, :, :].rearrange("a p t d -> p (a t) d"), resid[:, :, :]).then_inc(stored, 16)
            sp.wait_ge(stored, 16 * (PRIMED + B))
            for i in range(2):
                sp.wait_ge(w_in[i], 48 * (B * TURNS_B // 2 + 1))

        @block.tensor
        def _(pe):
            def unit(kind, i, bank, u, side, post):
                w = work[u % 2]
                pe.wait_ge(work_free[u % 2], PRIMED + bank + u // 2)
                if kind in ("k", "q", "v"):
                    par = side.par
                    if kind == "k" and i == 0:
                        pe.wait_ge(w_in[par], side.w_count)
                    wt = {"k": wk, "q": wq, "v": wv}[kind][par]
                    src, n_c = (hT, XC) if kind == "q" else (cT, CC)
                    if side.layer == 0 and kind != "v":
                        for c in range(n_c):
                            mm = pe.matmul(w[:, :], wt[:, c, :], src[:, c, tokens(i)], start=(c == 0), stop=(c == n_c - 1))
                    else:
                        for t in range(4):
                            for c in range(n_c):
                                mm = pe.matmul(w[:, tile(t)], src[:, c, tile(4 * i + t)], wt[:, c, :], start=(c == 0), stop=(c == n_c - 1))
                elif kind == "rowmax":
                    if i == 0:
                        wait_unit_evacuated(pe, bank, u - 1)
                    h, qt, n = i // (TT * NH), i // NH % TT, i % NH
                    mm = pe.matmul(w[:, :], q_high[side.par][h][:, tile(qt)], k_parts[side.par][h][:, tokens(n)], start=True, stop=True)
                elif kind == "shift":
                    h, n = i // NH, i % NH
                    if n == 0:
                        pe.wait_ge(neg_max_ok, G0 * side.sides + h + 1)
                    for t in range(4):
                        qt = 4 * n + t
                        mm = pe.matmul(w[0:1, tile(t)], neg_max[:, h, qt:qt + 1], ident_r[:, :], start=True, stop=True)
                elif kind in ("turn_k", "turn_q"):
                    which = ("turn_k", "turn_q").index(kind)
                    if i == 0:
                        pe.wait_ge(rope_step, ROPE_STEPS * (2 * side.sides + which + 1))
                    for t in range(TT):
                        mm = pe.transpose(work_h[u % 2][:, tile(t)], stack[which][:, t * G1 + i, :, :].rearrange("p a d -> p (a d)"), ident_h[:, :])
                elif kind == "den":
                    if i == 0:
                        pe.wait_ge(add_ok, post.adds)
                    g, d = ((G0, D0), (G1, D1))[post.layer]
                    for h in range(g):
                        mm = pe.matmul(w[h * d:(h + 1) * d, :], ones[post.layer][:, 0:d], acc[h][:, tokens(i)], start=True, stop=True)
                elif kind == "out":
                    if i == 0:
                        pe.wait_ge(o_norm_ok, PRIMED + post.turns)
                        pe.wait_ge(wo_in[post.par], post.w_count)
                    mm = pe.matmul(w[:, :], o_norm[:, tile(i)], wo[post.par][:, :], start=True, stop=True)
                mm.then_inc(work_full, 1)

            def score(l, t, par, kt, h, first):
                s = kt * (G0, G1)[l] + h
                if not (first and s < 2):
                    pe.wait_ge(exp_ok, t.steps + s - 1)
                for n in range(NH):
                    o = scores[s % 2][:, tokens(n)]
                    if l == 0:
                        pe.matmul(o, k_parts[par][h][:, tile(kt)], q_high[par][h][:, tokens(n)], start=True, stop=False)
                        mm = pe.matmul(o, k_one[par][h][:, tile(kt)], q_low[par][h][:, tokens(n)], start=False, stop=True)
                    else:
                        mm = pe.matmul(o, kT[par][:, h, tile(kt)], qT[par][:, h, tokens(n)], start=True, stop=True)
                mm.then_inc(scores_ok, 1)

            def attend(l, t, par, kt, n):
                g, d = ((G0, D0), (G1, D1))[l]
                if n == 0:
                    pe.wait_ge(exp_ok, t.steps + (kt + 1) * g)
                    if kt == 0:
                        pe.wait_ge(o_copied, PRIMED + t.turns)
                for h in range(g):
                    mm = pe.matmul(o_acc[h * d:(h + 1) * d, tokens(n)], v_tok[par][:, kt, h * d:(h + 1) * d],
                                   probs[:, (kt * g + h) % RING, tokens(n)], start=(kt == 0), stop=(kt == KT - 1))
                if n == NH - 1:
                    mm.then_inc(av_ok, 1)

            def one_turn(l, b, p, par, first, last, j=None):
                t = Counts(b, l, p)
                side, post = sides_of(b, l, p, par, j)
                g = (G0, G1)[l]
                wait_all_evacuated(pe, t.bank)
                if l == 0:
                    pe.wait_ge(dup_ok, NH * (t.sides + 1))
                for h in range(g if l == 0 else 2):
                    score(l, t, par, 0, h, first)
                if l == 1:
                    for h in range(2, g):
                        score(l, t, par, 0, h, first)
                u = 0
                for kt in range(KT):
                    for kind, i in chunk(l, kt, not last, not first):
                        unit(kind, i, t.bank, u, side, post)
                        u += 1
                    more = kt + 1 < KT
                    if more:
                        score(l, t, par, kt + 1, 0, False)
                        score(l, t, par, kt + 1, 1, False)
                    attend(l, t, par, kt, 0)
                    if more and l == 1:
                        score(l, t, par, kt + 1, 2, False)
                    attend(l, t, par, kt, 1)
                    if more and l == 1:
                        score(l, t, par, kt + 1, 3, False)

            def transposes(bank, u, src, n_c, ready):
                for c in range(n_c):
                    for n in range(NH):
                        pe.wait_ge(work_free[u % 2], PRIMED + bank + u // 2)
                        if ready is not None and c == 0:
                            pe.wait_ge(xn_ok, ready + 4 * (n + 1))
                        for t in range(4):
                            mm = pe.transpose(work[u % 2][:, tile(t)], src[:, 4 * n + t, tile(c)], ident[:, :])
                        mm.then_inc(work_full, 1)
                        u += 1
                return u

            pe.wait_ge(consts_in, 16 * 7)
            pe.wait_ge(consts_ok, 1)
            with pe.Fori(0, B) as b:
                start = b * (BATCH_UNITS // 2)
                pe.wait_ge(c_in, 16 * (b + 1))
                u = transposes(start, 0, c_raw, CC, None)
                transposes(start, u, xn, XC, 2 * TT * b)
                run_layer(pe, b, 0, unit, one_turn)
                transposes(side0_start(b, 1) - MID_UNITS // 2, 0, xn, XC, 2 * TT * b + TT)
                run_layer(pe, b, 1, unit, one_turn)

        @block.scalar
        def _(act):
            def unit(kind, i, bank, u, side, post):
                w = work[u % 2]
                full = 2 * bank + u + 1
                if kind in ("k", "q") and side.layer == 0:
                    act.wait_ge(work_full, full)
                    for h in range(G0):
                        dst = (k_parts if kind == "k" else q_high)[side.par][h]
                        a = act.activation(dst[0:D0, tokens(i)], w[h * D0:(h + 1) * D0, :], ACT.Copy)
                        if kind == "q":
                            a = act.activation(dst[D0:P, tokens(i)], w[h * D0:(h + 1) * D0, :], ACT.Copy)
                    a.then_inc(high_ok, 1)
                elif kind in ("k", "q"):
                    act.wait_ge(work_full, full)
                    act.activation(raw[kind == "q"][:, 4 * i:4 * i + 4, :, :].rearrange("p t h d -> p (t h d)"), w[:, :], ACT.Copy).then_inc(work_free[u % 2], 1)
                elif kind == "v":
                    act.wait_ge(work_full, full)
                    act.activation(v_tok[side.par][:, 4 * i:4 * i + 4, :].rearrange("p t d -> p (t d)"), w[:, :], ACT.Copy).then_inc(work_free[u % 2], 1)
                elif kind == "shift":
                    h, n = i // NH, i % NH
                    act.wait_ge(work_full, full)
                    act.activation(q_low[side.par][h][D0:D0 + 1, tokens(n)], w[0:1, :], ACT.Copy).then_inc(work_free[u % 2], 1)
                elif kind == "turn_q":
                    act.wait_ge(work_full, full)
                    act.activation(qT[side.par][:, i, :], work_h[u % 2], ACT.Copy).then_inc(work_free[u % 2], 1)

            def one_turn(l, b, p, par, first, last, j=None):
                t = Counts(b, l, p)
                side, post = sides_of(b, l, p, par, j)
                g = (G0, G1)[l]
                back = RING // g
                u = 0
                for kt in range(KT):
                    for h in range(g):
                        s = kt * g + h
                        old = kt - back
                        if old >= 0:
                            act.wait_ge(av_ok, t.avs + old + 1)
                            act.wait_ge(add_ok, t.adds + (max(old, 1) - 1) * g + h + 1)
                        elif not first:
                            act.wait_ge(av_ok, t.avs + old + 1)
                            act.wait_ge(add_ok, t.adds + old * g + h + 1)
                        act.wait_ge(scores_ok, t.steps + s + 1)
                        act.activation(probs[:, s % RING, :], scores[s % 2][:, :], ACT.Exp,
                                       scale=(1.0, float(D1) ** 0.5 / QK_SCALE ** 2)[l]).then_inc(exp_ok, 1)
                    for kind, i in chunk(l, kt, not last, not first):
                        unit(kind, i, t.bank, u, side, post)
                        u += 1
                act.wait_ge(o_norm_ok, PRIMED + t.turns)
                act.wait_ge(av_ok, t.avs + KT)
                act.activation(o_raw[:, :], o_acc[:, :], ACT.Copy).then_inc(o_copied, 1)

            def evacuate(bank, u, dst, n_c, scale, bias):
                for c in range(n_c):
                    for n in range(NH):
                        act.wait_ge(work_full, 2 * bank + u + 1)
                        if scale is None:
                            a = act.activation(dst[:, c, tokens(n)], work[u % 2][:, :], ACT.Copy)
                        else:
                            a = act.activation(dst[:, c, tokens(n)], work[u % 2][:, :], ACT.Identity,
                                               scale=affine[:, scale, c:c + 1],
                                               bias=0.0 if bias is None else affine[:, bias, c:c + 1])
                        a.then_inc(work_free[u % 2], 1)
                        u += 1
                return u

            act.wait_ge(consts_in, 16 * 7)
            with act.Fori(0, B) as b:
                start = b * (BATCH_UNITS // 2)
                u = evacuate(start, 0, cT, CC, None, None)
                evacuate(start, u, hT, XC, 0, 1)
                run_layer(act, b, 0, unit, one_turn)
                evacuate(side0_start(b, 1) - MID_UNITS // 2, 0, hT, XC, 2, None)
                run_layer(act, b, 1, unit, one_turn)

        @block.vector
        def _(dve):
            def unit(kind, i, bank, u, side, post):
                w = work[u % 2]
                full = 2 * bank + u + 1
                if kind in ("k", "q") and side.layer == 0:
                    dve.wait_ge(work_full, full)
                    dve.wait_ge(high_ok, 4 * side.sides + 2 * (kind == "q") + i + 1)
                    for h in range(G0):
                        hi = (k_parts if kind == "k" else q_high)[side.par][h][0:D0, tokens(i)].bitcast(F32)
                        lo = k_parts[side.par][h][D0:P, tokens(i)] if kind == "k" else q_low[side.par][h][0:D0, tokens(i)]
                        v = dve.tensor_tensor(lo, w[h * D0:(h + 1) * D0, :], hi, ALU.subtract)
                    v.then_inc(work_free[u % 2], 1)
                elif kind == "rowmax":
                    h, qt, n = i // (TT * NH), i // NH % TT, i % NH
                    dve.wait_ge(work_full, full)
                    dve.tensor_reduce(tile_max[:, h, qt, n:n + 1], w[:, :], AX.X, ALU.max, negate=True).then_inc(work_free[u % 2], 1)
                    if i % (TT * NH) == TT * NH - 1:
                        for k in range(2):
                            wait_unit_evacuated(dve, bank, u - k)
                        dve.tensor_reduce(neg_max[:, h, :], tile_max[:, h, :, :], AX.X, ALU.min).then_inc(neg_max_ok, 1)
                elif kind == "turn_k":
                    dve.wait_ge(work_full, full)
                    dve.tensor_copy(kT[side.par][:, i, :], work_h[u % 2]).then_inc(work_free[u % 2], 1)
                elif kind == "den":
                    dve.wait_ge(work_full, full)
                    dve.reciprocal(recip[:, tokens(i)], w[:, :]).then_inc(work_free[u % 2], 1)
                    if i == NH - 1:
                        for k in range(2):
                            wait_unit_evacuated(dve, bank, u - k)
                        dve.wait_ge(o_copied, PRIMED + post.turns)
                        dve.tensor_tensor(o_norm[:, :], o_raw[:, :], recip[:, :], ALU.mult).then_inc(o_norm_ok, 1)
                elif kind == "out":
                    if i == 0:
                        dve.wait_ge(bias_ok, post.b + 1)
                    dve.wait_ge(work_full, full)
                    dve.tensor_tensor(resid[:, i, :], w[:, :], resid[:, i, :], ALU.add).then_inc(work_free[u % 2], 1)

            def norms(kt, side, bank, post):
                for which, at in ((0, 2), (1, 4)):
                    n = 2 * side.sides + which
                    if kt == at:
                        dve.wait_ge(rope_step, ROPE_STEPS * n + 5)
                        dve.tensor_reduce(sumsq[:, :], tmp[:, :, :, :].rearrange("p t h d -> p (t h) d"), AX.X, ALU.add).then_inc(norm_step, 1)
                        dve.wait_ge(norm_step, NORM_STEPS * n + 1)
                        dve.tensor_scalar(sumsq[:, :], sumsq[:, :], L2_EPS ** 2, QK_SCALE ** -2, ALU.max, ALU.mult).then_inc(norm_step, 1)
                    if kt == at + 1:
                        dve.wait_ge(rope_step, ROPE_STEPS * n + 8)
                        a, c = ((2, 0), (1, 0))[which]
                        dve.tensor_tensor(stack[which][:, :, a, :], rot[:, :, :, :].rearrange("p t h d -> p (t h) d"),
                                          stack[which][:, :, c, :], ALU.subtract).then_inc(norm_step, 1)

            def one_turn(l, b, p, par, first, last, j=None):
                t = Counts(b, l, p)
                side, post = sides_of(b, l, p, par, j)
                g = (G0, G1)[l]
                u = 0
                for kt in range(KT):
                    for h in range(g if kt else 0):
                        s = kt * g + h
                        dve.wait_ge(exp_ok, t.steps + s + 1)
                        if kt > 1:
                            dve.wait_ge(add_ok, t.adds + (kt - 2) * g + h + 1)
                        before = probs[:, s - g, :] if kt == 1 else acc[h][:, :]
                        dve.tensor_tensor(acc[h][:, :], before, probs[:, s % RING, :], ALU.add).then_inc(add_ok, 1)
                    for kind, i in chunk(l, kt, not last, not first):
                        unit(kind, i, t.bank, u, side, post)
                        u += 1
                    if l == 1 and not last:
                        norms(kt, side, t.bank, not first)

            def row_norm(l, b):
                n = 2 * b + l
                for t in range(TT):
                    v = dve.bn_stats(stats[:, t, :], resid[:, t, :])
                v.then_inc(bn_ok, 1)
                dve.wait_ge(bn_ok, n + 1)
                dve.memset(gate_v[:, 0:1], 0.0)
                for t in range(TT):
                    v = dve.bn_aggr(mv[:, t, :], stats[:, t, :])
                v.then_inc(aggr_ok, 1)
                dve.wait_ge(aggr_ok, n + 1)
                if l == 0:
                    dve.tensor_scalar(var_eps[:, :], mv[:, :, 1], LN_EPS, None, ALU.add).then_inc(var_ok, 1)
                else:
                    dve.tensor_tensor(mean_sq[:, :], mv[:, :, 0], mv[:, :, 0], ALU.mult).then_inc(mean_sq_step, 1)
                    dve.wait_ge(mean_sq_step, 2 * b + 1)
                    dve.tensor_tensor(mean_sq[:, :], mean_sq[:, :], mv[:, :, 1], ALU.add).then_inc(mean_sq_step, 1)
                    dve.wait_ge(mean_sq_step, 2 * b + 2)
                    dve.tensor_scalar(var_eps[:, :], mean_sq[:, :], RMS_EPS, None, ALU.add).then_inc(var_ok, 1)
                dve.wait_ge(rstd_ok, 2 * b + l + 1)
                for t in range(TT):
                    if l == 0:
                        v = dve.tensor_scalar(xn[:, t, :], resid[:, t, :], mv[:, t, 0:1], rstd[:, t:t + 1], ALU.subtract, ALU.mult)
                    else:
                        v = dve.tensor_scalar(xn[:, t, :], resid[:, t, :], rstd[:, t:t + 1], None, ALU.mult)
                    v.then_inc(xn_ok, 1)

            for n, counter in enumerate((work_free[0], work_free[1], o_copied, o_norm_ok)):
                dve.memset(gate_v[:, 1 + n:2 + n], 0.0).then_inc(counter, PRIMED)
            dve.memset(gate_v[:, 5:6], 0.0).then_inc(stored, 16 * PRIMED)
            dve.memset(ones[0][:, :], float(D0) ** 0.5)
            dve.memset(ones[1][:, :], 1.0)
            dve.wait_ge(consts_in, 16 * 7)
            dve.tensor_copy(ident_r[:, :], ident[:, :])
            dve.tensor_copy(ident_h[:, :], ident[:, :]).then_inc(consts_ok, 1)
            with dve.Fori(0, B) as b:
                dve.wait_ge(x_in, 16 * (b + 1))
                for i in range(2):
                    for h in range(G0):
                        dve.memset(k_one[i][h][D0:D0 + 1, :].bitcast(F32), 1.0)
                row_norm(0, b)
                run_layer(dve, b, 0, unit, one_turn)
                wait_all_evacuated(dve, side0_start(b, 1) - MID_UNITS // 2)
                row_norm(1, b)
                run_layer(dve, b, 1, unit, one_turn, norms)

        @block.gpsimd
        def _(pool):
            def unit(kind, i, bank, u, side, post):
                if kind == "k" and side.layer == 0:
                    pool.wait_ge(high_ok, 4 * side.sides + i + 1)
                    pool.tensor_tensor(gate_p[:, i:i + 1], power[:, 0:1], power[:, 0:1], ALU.mult)
                    for h in range(G0):
                        c = pool.tensor_copy(k_one[side.par][h][0:D0, tokens(i)], k_parts[side.par][h][0:D0, tokens(i)].bitcast(F32))
                    c.then_inc(dup_ok, 1)

            def rope(which, side, bank, u):
                n = ROPE_STEPS * (2 * side.sides + which)
                wait_unit_evacuated(pool, bank, u - 2)
                wait_unit_evacuated(pool, bank, u - 1)
                r, half = raw[which], D1 // 2
                c4 = cos[:, :, :].unsqueeze(2).broadcast_to([P, TT, G1, D1])
                s4 = sin[:, :, :].unsqueeze(2).broadcast_to([P, TT, G1, D1])
                if which == 1:
                    pool.wait_ge(norm_step, NORM_STEPS * (2 * side.sides + 1))
                pool.tensor_tensor(rot[:, :, :, :], r[:, :, :, :], c4, ALU.mult).then_inc(rope_step, 1)
                pool.tensor_tensor(tmp[:, :, :, 0:half], r[:, :, :, half:D1], s4[:, :, :, 0:half], ALU.mult).then_inc(rope_step, 1)
                pool.tensor_tensor(tmp[:, :, :, half:D1], r[:, :, :, 0:half], s4[:, :, :, half:D1], ALU.mult).then_inc(rope_step, 1)
                pool.wait_ge(rope_step, n + 3)
                pool.tensor_tensor(rot[:, :, :, :], rot[:, :, :, :], tmp[:, :, :, :], ALU.add).then_inc(rope_step, 1)
                pool.wait_ge(rope_step, n + 4)
                pool.tensor_tensor(tmp[:, :, :, :], rot[:, :, :, :], rot[:, :, :, :], ALU.mult).then_inc(rope_step, 1)

            def scale_and_split(which, side):
                n = ROPE_STEPS * (2 * side.sides + which)
                m = NORM_STEPS * (2 * side.sides + which)
                vec = rot[:, :, :, :].rearrange("p t h d -> p (t h) d")
                pool.wait_ge(norm_step, m + 2)
                pool.tensor_tensor(inv[:, :], sumsq[:, :], power[:, :], ALU.pow).then_inc(rope_step, 1)
                pool.wait_ge(rope_step, n + 6)
                pool.tensor_tensor(vec, vec, inv[:, :].unsqueeze(2).broadcast_to([P, TT * G1, D1]), ALU.mult).then_inc(rope_step, 1)
                pool.wait_ge(rope_step, n + 7)
                g = 4 + which
                pool.tensor_tensor(gate_p[:, g:g + 1], power[:, 0:1], power[:, 0:1], ALU.mult)
                pool.tensor_copy(stack[which][:, :, 0, :], vec).then_inc(rope_step, 1)
                pool.wait_ge(rope_step, n + 8)
                g = 6 + which
                pool.tensor_tensor(gate_p[:, g:g + 1], power[:, 0:1], power[:, 0:1], ALU.mult)
                pool.tensor_copy(stack[which][:, :, (1, 2)[which], :], stack[which][:, :, 0, :]).then_inc(rope_step, 1)
                pool.wait_ge(norm_step, m + 3)
                g = 8 + which
                pool.tensor_tensor(gate_p[:, g:g + 1], power[:, 0:1], power[:, 0:1], ALU.mult)
                pool.tensor_copy(stack[which][:, :, 3, :], stack[which][:, :, (2, 1)[which], :]).then_inc(rope_step, 1)

            def rotations(kt, side, bank, post):
                ends = [sum(len(chunk(1, c, True, post)) for c in range(n + 1)) for n in range(2)]
                if kt == 1:
                    rope(0, side, bank, ends[0])
                if kt == 2:
                    scale_and_split(0, side)
                if kt == 3:
                    rope(1, side, bank, ends[1])
                if kt == 4:
                    scale_and_split(1, side)

            def one_turn(l, b, p, par, first, last, j=None):
                t = Counts(b, l, p)
                side, post = sides_of(b, l, p, par, j)
                u = 0
                for kt in range(0 if last else KT):
                    for kind, i in chunk(l, kt, True, not first):
                        unit(kind, i, t.bank, u, side, post)
                        u += 1
                    if l == 1:
                        rotations(kt, side, t.bank, not first)

            def row_power(n):
                pool.wait_ge(var_ok, n + 1)
                pool.tensor_tensor(rstd[:, :], var_eps[:, :], power[:, 0:TT], ALU.pow).then_inc(rstd_ok, 1)

            pool.memset(power[:, :], -0.5).then_inc(power_ok, 1)
            pool.wait_ge(power_ok, 1)
            pool.wait_ge(consts_in, 16 * 7)
            with pool.Fori(0, B) as b:
                row_power(2 * b)
                pool.wait_ge(xn_ok, 2 * TT * b + TT)
                pool.tensor_tensor(resid[:, :, :], resid[:, :, :], bo_all[:, :].unsqueeze(1).broadcast_to([P, TT, D]), ALU.add).then_inc(bias_ok, 1)
                run_layer(pool, b, 0, unit, one_turn)
                row_power(2 * b + 1)
                run_layer(pool, b, 1, unit, one_turn, rotations)


_INS = ['x', 'ctx_768', 'L0_xattn_Wq', 'L0_xattn_Wk', 'L0_xattn_Wv', 'L0_xattn_Wo', 'L0_xattn_bo', 'L0_xattn_gamma',
        'L0_xattn_beta', 'L1_xattn_norm_w', 'L1_xattn_wq', 'L1_xattn_wkv', 'L1_xattn_wout']
_OUTS = [((B, S, D), 'float32')]


def rope_tables():
    inv_freq = 1.0 / 10000.0 ** (np.arange(0, D1, 2, dtype=np.float32) / D1)
    freqs = np.einsum('i,j->ij', np.arange(S, dtype=np.float32), inv_freq)
    emb = np.concatenate([freqs, freqs], axis=-1)
    sign = np.where(np.arange(D1) < D1 // 2, -1.0, 1.0)
    return np.cos(emb).astype(np.float32), (np.sin(emb) * sign).astype(np.float32)


def kernel(**inputs):
    import numpy as _np
    import concourse.bacc as _bacc
    from concourse import mybir as _mybir
    from concourse.bass_utils import run_bass_kernel_spmd as _run

    nc = _bacc.Bacc("TRN2", target_bir_lowering=False, num_devices=1)
    arrays, args = {}, []
    given = {name: _np.ascontiguousarray(inputs[name]) for name in _INS}
    given["cos"], given["sin"] = rope_tables()
    given["ident"] = _np.eye(P, dtype=_np.float32)
    for name, a in given.items():
        arrays[f"in_{name}_dram"] = a
        args.append(nc.dram_tensor(f"in_{name}_dram", a.shape, _mybir.dt.from_np(a.dtype), kind="ExternalInput").ap())
    for i, (shape, dtype) in enumerate(_OUTS):
        dt = _mybir.dt.from_np(_np.dtype(dtype))
        args.append(nc.dram_tensor(f"out_{i}_dram", shape, dt, kind="ExternalOutput").ap())
    build(nc, *args)
    r = _run(nc, [arrays], core_ids=[0])
    got = tuple(r.results[0][f"out_{i}_dram"] for i in range(len(_OUTS)))
    return got[0]
```

```python
from contextlib import ExitStack

import numpy as np

import concourse.bass as bass
from concourse import mybir

F32 = mybir.dt.float32
F32R = mybir.dt.float32r
F16 = mybir.dt.float16
ALU = mybir.AluOpType
ACT = mybir.ActivationFunctionType
AX = mybir.AxisListType

B, S, D, DC = 4, 1024, 512, 384
P = 128
TT = S // P
NH = S // 512
XC, CC = D // P, DC // P
HEADS = 16
D0, D1 = 64, D // HEADS
G0, G1 = P // D0, P // D1
TURNS0, TURNS1 = HEADS // G0, HEADS // G1
KT = S // P
LN_EPS = RMS_EPS = 1e-5
L2_EPS = 1e-12
QK_SCALE = 64.0
PRIMED = 1
RING = 8


def _x(a, b):
    return [("rowmax", i) for i in range(a, b)]


SIDE0 = [[("k", 0), ("k", 1)], [("q", 0), ("q", 1)], _x(0, 5), _x(5, 11), _x(11, 17),
         _x(17, 23) + [("shift", 0), ("shift", 1)], _x(23, 29) + [("v", 0)],
         _x(29, 32) + [("v", 1), ("shift", 2), ("shift", 3)]]
SIDE1 = [[("k", 0), ("k", 1)], [("q", 0), ("q", 1)], [("v", 0), ("v", 1)], [], [], [],
         [("turn_k", h) for h in range(G1)], [("turn_q", h) for h in range(G1)]]
POST = [[("den", 0), ("den", 1)], [], [("out", 0), ("out", 1)], [("out", 2), ("out", 3)],
        [("out", 4), ("out", 5)], [("out", 6), ("out", 7)], [], []]


def chunk(layer, kt, side, post):
    return (POST[kt] if post else []) + ((SIDE0, SIDE1)[layer][kt] if side else [])


def share(items, part, parts):
    return items[part * len(items) // parts:(part + 1) * len(items) // parts]


def n_units(layer, side, post):
    return sum(len(chunk(layer, kt, side, post)) for kt in range(KT))


PREP_UNITS = (CC + XC) * NH
MID_UNITS = XC * NH
TURNS = (TURNS0, TURNS1)
STEPS = (KT * G0, KT * G1)
ADDS = ((KT - 1) * G0, (KT - 1) * G1)
BODY = tuple(n_units(l, True, True) for l in (0, 1))
FIRST = tuple(n_units(l, True, False) for l in (0, 1))
LAST = n_units(0, False, True)


def layer_units(l):
    return 2 * FIRST[l] + (TURNS[l] - 2) * BODY[l] + 2 * LAST


BATCH_UNITS = PREP_UNITS + layer_units(0) + MID_UNITS + layer_units(1)
TURNS_B = sum(TURNS)


def side0_start(b, l):
    return b * (BATCH_UNITS // 2) + (PREP_UNITS + l * (layer_units(0) + MID_UNITS)) // 2


class Counts:

    def __init__(self, b, l, p):
        self.bank = side0_start(b, l) + FIRST[l] // 2
        if not (isinstance(p, int) and p == 0):
            self.bank = self.bank + FIRST[l] // 2 + (p - 1) * (BODY[l] // 2)
        self.turns = b * TURNS_B + l * TURNS0 + p
        self.avs = self.turns * KT
        self.steps = (b * (TURNS0 * STEPS[0] + TURNS1 * STEPS[1]) + l * TURNS0 * STEPS[0]
                      + p * STEPS[l])
        self.adds = (b * (TURNS0 * ADDS[0] + TURNS1 * ADDS[1]) + l * TURNS0 * ADDS[0]
                     + p * ADDS[l])
        self.sides = b * TURNS[l] + p


class Share:

    def __init__(self, b, layer, par, turns, adds, sides, w_count):
        self.b, self.layer, self.par = b, layer, par
        self.turns, self.adds, self.sides, self.w_count = turns, adds, sides, w_count


def build(nc, rows, x, ctx_in, wq0, wk0, wv0, wo0, bo, gamma, beta, norm_w, wq1, wkv1, wout1,
          cos_t, sin_t, ident_t, out):
    W0 = {"q": wq0.rearrange("(c p) n -> p c n", p=P), "k": wk0.rearrange("(c p) n -> p c n", p=P),
          "v": wv0.rearrange("(c p) n -> p c n", p=P), "o": wo0}
    kv1 = wkv1.rearrange("(c p) n -> p c n", p=P)
    W1 = {"q": wq1.rearrange("(c p) n -> p c n", p=P), "k": kv1[:, :, 0:D], "v": kv1[:, :, D:2 * D],
          "o": wout1}
    WEIGHTS = (W0, W1)
    x_rows = x.rearrange("b (t p) d -> b p t d", p=P)
    c_rows = ctx_in.rearrange("b (t p) d -> b p t d", p=P)
    out_rows = out.rearrange("b (t p) d -> b p t d", p=P)

    with ExitStack() as ctx:
        def sb(name, shape, dt=F32, scope=ctx):
            return scope.enter_context(nc.sbuf_tensor(name, shape, dt))

        def sem(name):
            return ctx.enter_context(nc.semaphore(name))

        ident = sb("ident", [P, P])
        ident_r = sb("ident_r", [P, P], F32R)
        ident_h = sb("ident_h", [P, P], F16)
        ones = [sb("ones_scaled", [P, D0]), sb("ones_plain", [P, D0])]
        cos = sb("cos", [P, TT, D1])
        sin = sb("sin", [P, TT, D1])
        affine = sb("affine", [P, 3, XC])
        bo_all = sb("bo_all", [P, D])
        stats = sb("stats", [P, TT, 6])
        mv = sb("mv", [P, TT, 2])
        var_eps = sb("var_eps", [P, TT])
        mean_sq = sb("mean_sq", [P, TT])
        rstd = sb("rstd", [P, TT])
        gate_v = sb("gate_v", [P, 6])
        gate_p = sb("gate_p", [P, NH])
        power = sb("power", [P, TT * G1])
        resid = sb("resid", [P, TT, D])
        hT = sb("hT", [P, XC, S])
        cT = sb("cT", [P, CC, S])
        wq = [sb(f"wq{i}", [P, XC, P]) for i in range(2)]
        wk = [sb(f"wk{i}", [P, CC, P]) for i in range(2)]
        wv = [sb(f"wv{i}", [P, CC, P]) for i in range(2)]
        wo = [sb(f"wo{i}", [P, D]) for i in range(2)]
        v_tok = [sb(f"v_tok{i}", [P, KT, P]) for i in range(2)]
        probs = sb("probs", [P, RING, S])
        acc = [sb(f"acc{h}", [P, S]) for h in range(G1)]
        o_raw = sb("o_raw", [P, S])
        recip = sb("recip", [P, S])
        den_t = sb("den_t", [P, G1, TT])
        recip_t = sb("recip_t", [P, G1, TT])
        o_norm = sb("o_norm", [P, S])
        xn = probs[:, 0:4, :].rearrange("p a b -> p (a b)").rearrange("p (t d) -> p t d", d=D)
        c_raw = probs[:, 4:7, :].rearrange("p a b -> p (a b)").rearrange("p (t d) -> p t d", d=DC)

        with ExitStack() as scope:
            k_parts = [[sb(f"k_parts{i}{h}", [P, S], F32R, scope) for h in range(G0)] for i in range(2)]
            k_one = [[sb(f"k_one{i}{h}", [D0 + 1, S], F32R, scope) for h in range(G0)] for i in range(2)]
            q_high = [[sb(f"q_high{i}{h}", [P, S], F32R, scope) for h in range(G0)] for i in range(2)]
            q_low = [[sb(f"q_low{i}{h}", [D0 + 1, S], F32R, scope) for h in range(G0)] for i in range(2)]
            tile_max = sb("tile_max", [P, G0, TT, NH], F32, scope)
            neg_max = sb("neg_max", [P, G0, TT], F32R, scope)
        with ExitStack() as scope:
            kT = [sb(f"kT{i}", [P, G1, S], F16, scope) for i in range(2)]
            qT = [sb(f"qT{i}", [P, G1, S], F16, scope) for i in range(2)]
            stack = [sb(f"stack{n}", [P, TT * G1, 4, D1], F16, scope) for n in ("k", "q")]
            raw = [sb(f"raw{n}", [P, TT, G1, D1], F32, scope) for n in ("k", "q")]
            rot = sb("rot", [P, TT, G1, D1], F32, scope)
            tmp = sb("tmp", [P, TT, G1, D1], F32, scope)
            squares = sb("squares", [P, TT * G1, D1], F32, scope)
            sumsq = sb("sumsq", [P, 2, TT * G1], F32, scope)
            inv = sb("inv", [P, 2, TT * G1], F32, scope)

        scores = [ctx.enter_context(nc.psum_tensor(f"scores{i}", [P, S], F32)) for i in range(2)]
        o_acc = ctx.enter_context(nc.psum_tensor("o_acc", [P, S], F32))
        work = [ctx.enter_context(nc.psum_tensor(f"work{i}", [P, 512], F32)) for i in range(2)]
        work_h = [w[:, :].bitcast(F16) for w in work]

        consts_in = sem("consts_in")
        consts_ok = sem("consts_ok")
        x_in = sem("x_in")
        c_in = sem("c_in")
        w_in = [sem(f"w_in{i}") for i in range(2)]
        wo_in = [sem(f"wo_in{i}") for i in range(2)]
        stored = sem("stored")
        bn_ok = sem("bn_ok")
        aggr_ok = sem("aggr_ok")
        mean_sq_step = sem("mean_sq_step")
        var_ok = sem("var_ok")
        rstd_ok = sem("rstd_ok")
        xn_ok = sem("xn_ok")
        bias_ok = sem("bias_ok")
        power_ok = sem("power_ok")
        work_full = sem("work_full")
        work_free = [sem(f"work_free{i}") for i in range(2)]
        high_ok = sem("high_ok")
        dup_ok = sem("dup_ok")
        neg_max_ok = sem("neg_max_ok")
        scores_ok = sem("scores_ok")
        exp_ok = sem("exp_ok")
        add_ok = sem("add_ok")
        av_ok = sem("av_ok")
        o_copied = sem("o_copied")
        o_norm_ok = sem("o_norm_ok")
        den_out = sem("den_out")
        den_in = sem("den_in")
        recip_ok = sem("recip_ok")
        recip_out = sem("recip_out")
        recip_in = sem("recip_in")
        high1_ok = sem("high1_ok")
        rope_step = sem("rope_step")
        norm_step = sem("norm_step")
        ROPE_STEPS, NORM_STEPS = 12, 12
        def sides_of(b, l, p, par, j=None):
            t = Counts(b, l, p)
            half_side, half_post = (j + 1, j) if j is not None else ((p + 1) // 2, (p - 1) // 2)
            loads = b * (TURNS_B // 2) + l * (TURNS0 // 2)
            side = Share(b, l, 1 - par, None, None, t.sides + 1, 16 * 3 * (loads + half_side + 1))
            post = Share(b, l, 1 - par, t.turns, t.adds, None, 16 * (loads + half_post + 1))
            return side, post

        def run_layer(eng, b, l, unit, one_turn, extra=None):
            side, _ = sides_of(b, l, -1, 1)
            u = 0
            for kt in range(KT):
                for kind, i in chunk(l, kt, True, False):
                    unit(kind, i, side0_start(b, l), u, side, None)
                    u += 1
                if extra is not None and l == 1:
                    extra(kt, side, side0_start(b, 1), False)
            one_turn(l, b, 0, 0, True, False)
            if l == 0:
                with eng.Fori(0, (TURNS0 - 2) // 2) as j:
                    for i in range(2):
                        one_turn(l, b, 2 * j + 1 + i, 1 - i, False, False, j)
            else:
                for p in range(1, TURNS1 - 1):
                    one_turn(l, b, p, p % 2, False, False)
            p = TURNS[l] - 1
            one_turn(l, b, p, p % 2, False, True)
            _, post = sides_of(b, l, p + 1, (p + 1) % 2)
            bank = Counts(b, l, p).bank + LAST // 2
            u = 0
            for kt in range(KT):
                for kind, i in chunk(l, kt, False, True):
                    unit(kind, i, bank, u, None, post)
                    u += 1

        block = ctx.enter_context(nc.Block())

        def wait_unit_evacuated(eng, bank, u):
            eng.wait_ge(work_free[u % 2], PRIMED + bank + (u // 2 + 1))

        def wait_all_evacuated(eng, bank):
            for i in range(2):
                eng.wait_ge(work_free[i], PRIMED + bank)

        def tokens(n):
            return slice(n * 512, (n + 1) * 512)

        def tile(t):
            return slice(t * P, (t + 1) * P)

        @block.sync
        def _(sp):
            for dst, src in ((ident[:, :], ident_t), (cos[:, :, :], cos_t.rearrange("(t p) d -> p t d", p=P)),
                             (sin[:, :, :], sin_t.rearrange("(t p) d -> p t d", p=P)),
                             (affine[:, 0, :], gamma.rearrange("(c p) -> p c", p=P)),
                             (affine[:, 1, :], beta.rearrange("(c p) -> p c", p=P)),
                             (affine[:, 2, :], norm_w.rearrange("(c p) -> p c", p=P)),
                             (bo_all[:, :], bo.rearrange("(a n) -> a n", a=1).to_broadcast([P, D]))):
                with nc.allow_non_contiguous_dma("small constants, once"):
                    sp.dma_start(dst, src).then_inc(consts_in, 16)

            def load_side(l, p, par):
                for name, dst in (("q", wq), ("k", wk), ("v", wv)):
                    sp.dma_start(dst[par][:, :, :], WEIGHTS[l][name][:, :, bass.ds(p * P, P)]).then_inc(w_in[par], 16)

            def load_out(l, p, par):
                sp.dma_start(wo[par][:, :], WEIGHTS[l]["o"][bass.ds(p * P, P), :]).then_inc(wo_in[par], 16)

            def after(b, l, p):
                sp.wait_ge(work_full, 2 * Counts(b, l, p).bank)

            def turn_sums(b, l, bank, turns):
                g, d = ((G0, D0), (G1, D1))[l]
                wait_unit_evacuated(sp, bank, 0)
                wait_unit_evacuated(sp, bank, 1)
                sp.dma_start(rows[0, 0:g, :], recip[0:(g - 1) * d + 1:d, :]).then_inc(den_out, 16)
                with nc.allow_non_contiguous_dma("runs of eight sums"):
                    sp.wait_ge(den_out, 16 * turns)
                    sp.dma_start(den_t[:, 0:g, :], rows[0, 0:g, :].rearrange("h (p j) -> p h j", j=TT)).then_inc(den_in, 16)
                    sp.wait_ge(recip_ok, turns)
                    sp.dma_start(rows[1, 0:g, :].rearrange("h (p j) -> p h j", j=TT), recip_t[:, 0:g, :]).then_inc(recip_out, 16)
                sp.wait_ge(recip_out, 16 * turns)
                for h in range(G1):
                    row = h * g // G1
                    sp.dma_start(recip[h * D1:(h + 1) * D1, :], rows[1, row:row + 1, :].to_broadcast([D1, S])).then_inc(recip_in, 16)

            load_side(0, 0, 0)
            load_side(0, 1, 1)
            with sp.Fori(0, B) as b:
                sp.wait_ge(stored, 16 * (PRIMED + b))
                sp.dma_start(c_raw, c_rows[bass.ds(b, 1), :, :, :].rearrange("a p t d -> p (a t) d")).then_inc(c_in, 16)
                sp.dma_start(resid[:, :, :], x_rows[bass.ds(b, 1), :, :, :].rearrange("a p t d -> p (a t) d")).then_inc(x_in, 16)
                after(b, 0, 0)
                load_out(0, 0, 0)
                load_side(0, 2, 0)
                with sp.Fori(0, (TURNS0 - 4) // 2) as j:
                    for i in range(2):
                        p = 2 * j + 1 + i
                        after(b, 0, p)
                        load_out(0, p, 1 - i)
                        load_side(0, p + 2, 1 - i)
                        turn_sums(b, 0, Counts(b, 0, p).bank, Counts(b, 0, p).turns)
                after(b, 0, TURNS0 - 3)
                load_out(0, TURNS0 - 3, 1)
                load_side(0, TURNS0 - 1, 1)
                turn_sums(b, 0, Counts(b, 0, TURNS0 - 3).bank, Counts(b, 0, TURNS0 - 3).turns)
                for p in (TURNS0 - 2, TURNS0 - 1):
                    after(b, 0, p)
                    load_out(0, p, p % 2)
                    load_side(1, p - (TURNS0 - 2), p % 2)
                    turn_sums(b, 0, Counts(b, 0, p).bank, Counts(b, 0, p).turns)
                turn_sums(b, 0, Counts(b, 0, TURNS0 - 1).bank + LAST // 2, Counts(b, 0, TURNS0).turns)
                for p in range(TURNS1):
                    after(b, 1, p)
                    load_out(1, p, p % 2)
                    if p < TURNS1 - 2:
                        load_side(1, p + 2, p % 2)
                    else:
                        load_side(0, p - (TURNS1 - 2), p % 2)
                    if p > 0:
                        turn_sums(b, 1, Counts(b, 1, p).bank, Counts(b, 1, p).turns)
                turn_sums(b, 1, Counts(b, 1, TURNS1 - 1).bank + LAST // 2, Counts(b, 1, TURNS1).turns)
                wait_all_evacuated(sp, (b + 1) * (BATCH_UNITS // 2))
                sp.dma_start(out_rows[bass.ds(b, 1), :, :, :].rearrange("a p t d -> p (a t) d"), resid[:, :, :]).then_inc(stored, 16)
            sp.wait_ge(stored, 16 * (PRIMED + B))
            for i in range(2):
                sp.wait_ge(w_in[i], 48 * (B * TURNS_B // 2 + 1))

        @block.tensor
        def _(pe):
            def unit(kind, i, bank, u, side, post):
                w = work[u % 2]
                pe.wait_ge(work_free[u % 2], PRIMED + bank + u // 2)
                if kind in ("k", "q", "v"):
                    par = side.par
                    if kind == "k" and i == 0:
                        pe.wait_ge(w_in[par], side.w_count)
                    wt = {"k": wk, "q": wq, "v": wv}[kind][par]
                    src, n_c = (hT, XC) if kind == "q" else (cT, CC)
                    if side.layer == 0 and kind != "v":
                        for c in range(n_c):
                            mm = pe.matmul(w[:, :], wt[:, c, :], src[:, c, tokens(i)], start=(c == 0), stop=(c == n_c - 1))
                    else:
                        for t in range(4):
                            for c in range(n_c):
                                mm = pe.matmul(w[:, tile(t)], src[:, c, tile(4 * i + t)], wt[:, c, :], start=(c == 0), stop=(c == n_c - 1))
                elif kind == "rowmax":
                    if i == 0:
                        wait_unit_evacuated(pe, bank, u - 1)
                    h, qt, n = i // (TT * NH), i // NH % TT, i % NH
                    mm = pe.matmul(w[:, :], q_high[side.par][h][:, tile(qt)], k_parts[side.par][h][:, tokens(n)], start=True, stop=True)
                elif kind == "shift":
                    h, n = i // NH, i % NH
                    if n == 0:
                        pe.wait_ge(neg_max_ok, G0 * side.sides + h + 1)
                    for t in range(4):
                        qt = 4 * n + t
                        mm = pe.matmul(w[0:1, tile(t)], neg_max[:, h, qt:qt + 1], ident_r[:, :], start=True, stop=True)
                elif kind in ("turn_k", "turn_q"):
                    which = ("turn_k", "turn_q").index(kind)
                    if i == 0:
                        pe.wait_ge(norm_step, NORM_STEPS * side.sides + (9, 12)[which])
                    for t in range(TT):
                        mm = pe.transpose(work_h[u % 2][:, tile(t)], stack[which][:, t * G1 + i, :, :].rearrange("p a d -> p (a d)"), ident_h[:, :])
                elif kind == "den":
                    if i == 0:
                        pe.wait_ge(add_ok, post.adds)
                    g, d = ((G0, D0), (G1, D1))[post.layer]
                    for h in range(g):
                        mm = pe.matmul(w[h * d:(h + 1) * d, :], ones[post.layer][:, 0:d], acc[h][:, tokens(i)], start=True, stop=True)
                elif kind == "out":
                    if i == 0:
                        pe.wait_ge(o_norm_ok, PRIMED + post.turns)
                        pe.wait_ge(wo_in[post.par], post.w_count)
                    mm = pe.matmul(w[:, :], o_norm[:, tile(i)], wo[post.par][:, :], start=True, stop=True)
                mm.then_inc(work_full, 1)

            def score(l, t, par, kt, h, first):
                s = kt * (G0, G1)[l] + h
                if not (first and s < 2):
                    pe.wait_ge(exp_ok, t.steps + s - 1)
                for n in range(NH):
                    o = scores[s % 2][:, tokens(n)]
                    if l == 0:
                        pe.matmul(o, k_parts[par][h][:, tile(kt)], q_high[par][h][:, tokens(n)], start=True, stop=False)
                        mm = pe.matmul(o, k_one[par][h][:, tile(kt)], q_low[par][h][:, tokens(n)], start=False, stop=True)
                    else:
                        mm = pe.matmul(o, kT[par][:, h, tile(kt)], qT[par][:, h, tokens(n)], start=True, stop=True)
                mm.then_inc(scores_ok, 1)

            def attend(l, t, par, kt, n):
                g, d = ((G0, D0), (G1, D1))[l]
                if n == 0:
                    pe.wait_ge(exp_ok, t.steps + (kt + 1) * g)
                    if kt == 0:
                        pe.wait_ge(o_copied, PRIMED + t.turns)
                for h in range(g):
                    mm = pe.matmul(o_acc[h * d:(h + 1) * d, tokens(n)], v_tok[par][:, kt, h * d:(h + 1) * d],
                                   probs[:, (kt * g + h) % RING, tokens(n)], start=(kt == 0), stop=(kt == KT - 1))
                if n == NH - 1:
                    mm.then_inc(av_ok, 1)

            def one_turn(l, b, p, par, first, last, j=None):
                t = Counts(b, l, p)
                side, post = sides_of(b, l, p, par, j)
                g = (G0, G1)[l]
                wait_all_evacuated(pe, t.bank)
                if l == 0:
                    pe.wait_ge(dup_ok, NH * (t.sides + 1))
                for h in range(g if l == 0 else 2):
                    score(l, t, par, 0, h, first)
                if l == 1:
                    for h in range(2, g):
                        score(l, t, par, 0, h, first)
                u = 0
                for kt in range(KT):
                    units = chunk(l, kt, not last, not first)
                    pieces = [("score", 0), ("score", 1), ("attend", 0), ("attend", 1)]
                    if l == 1:
                        pieces = [("score", 0), ("score", 1), ("attend", 0), ("score", 2), ("attend", 1), ("score", 3)]
                    if kt == KT - 1:
                        pieces = [("attend", 0), ("attend", 1)]
                    slots = min(3, len(pieces)) if l == 1 else len(pieces)
                    for n, (piece, which) in enumerate(pieces):
                        for kind, i in share(units, n, slots) if n < slots else []:
                            unit(kind, i, t.bank, u, side, post)
                            u += 1
                        if piece == "score":
                            score(l, t, par, kt + 1, which, False)
                        else:
                            attend(l, t, par, kt, which)

            def transposes(bank, u, src, n_c, ready):
                for c in range(n_c):
                    for n in range(NH):
                        pe.wait_ge(work_free[u % 2], PRIMED + bank + u // 2)
                        if ready is not None and c == 0:
                            pe.wait_ge(xn_ok, ready + 4 * (n + 1))
                        for t in range(4):
                            mm = pe.transpose(work[u % 2][:, tile(t)], src[:, 4 * n + t, tile(c)], ident[:, :])
                        mm.then_inc(work_full, 1)
                        u += 1
                return u

            pe.wait_ge(consts_in, 16 * 7)
            pe.wait_ge(consts_ok, 1)
            with pe.Fori(0, B) as b:
                start = b * (BATCH_UNITS // 2)
                pe.wait_ge(c_in, 16 * (b + 1))
                u = transposes(start, 0, c_raw, CC, None)
                transposes(start, u, xn, XC, 2 * TT * b)
                run_layer(pe, b, 0, unit, one_turn)
                transposes(side0_start(b, 1) - MID_UNITS // 2, 0, xn, XC, 2 * TT * b + TT)
                run_layer(pe, b, 1, unit, one_turn)

        @block.scalar
        def _(act):
            def unit(kind, i, bank, u, side, post):
                w = work[u % 2]
                full = 2 * bank + u + 1
                if kind in ("k", "q") and side.layer == 0:
                    act.wait_ge(work_full, full)
                    for h in range(G0):
                        dst = (k_parts if kind == "k" else q_high)[side.par][h]
                        a = act.activation(dst[0:D0, tokens(i)], w[h * D0:(h + 1) * D0, :], ACT.Copy)
                        if kind == "q":
                            a = act.activation(dst[D0:P, tokens(i)], w[h * D0:(h + 1) * D0, :], ACT.Copy)
                    a.then_inc(high_ok, 1)
                elif kind in ("k", "q"):
                    act.wait_ge(work_full, full)
                    act.activation(raw[kind == "q"][:, 4 * i:4 * i + 4, :, :].rearrange("p t h d -> p (t h d)"), w[:, :], ACT.Copy).then_inc(work_free[u % 2], 1)
                elif kind == "v":
                    act.wait_ge(work_full, full)
                    act.activation(v_tok[side.par][:, 4 * i:4 * i + 4, :].rearrange("p t d -> p (t d)"), w[:, :], ACT.Copy).then_inc(work_free[u % 2], 1)
                elif kind == "shift":
                    h, n = i // NH, i % NH
                    act.wait_ge(work_full, full)
                    act.activation(q_low[side.par][h][D0:D0 + 1, tokens(n)], w[0:1, :], ACT.Copy).then_inc(work_free[u % 2], 1)
                elif kind in ("turn_k", "turn_q"):
                    act.wait_ge(work_full, full)
                    dst = kT if kind == "turn_k" else qT
                    act.activation(dst[side.par][:, i, :], work_h[u % 2], ACT.Copy).then_inc(work_free[u % 2], 1)
                elif kind == "den":
                    if i == 0:
                        act.wait_ge(o_norm_ok, PRIMED + post.turns - 1)
                    act.wait_ge(work_full, full)
                    act.activation(recip[:, tokens(i)], w[:, :], ACT.Copy).then_inc(work_free[u % 2], 1)

            def highs(kt, side, bank, post):
                for which, at in ((0, 4), (1, 5)):
                    if kt == at:
                        act.wait_ge(rope_step, ROPE_STEPS * side.sides + (10, 12)[which])
                        act.activation(stack[which][:, :, 0, :], raw[which][:, :, :, :].rearrange("p t h d -> p (t h) d"), ACT.Copy).then_inc(high1_ok, 1)

            def one_turn(l, b, p, par, first, last, j=None):
                t = Counts(b, l, p)
                side, post = sides_of(b, l, p, par, j)
                g = (G0, G1)[l]
                back = RING // g
                u = 0
                for kt in range(KT):
                    for h in range(g):
                        s = kt * g + h
                        old = kt - back
                        if old >= 0:
                            act.wait_ge(av_ok, t.avs + old + 1)
                            act.wait_ge(add_ok, t.adds + (max(old, 1) - 1) * g + h + 1)
                        elif not first:
                            act.wait_ge(av_ok, t.avs + old + 1)
                            act.wait_ge(add_ok, t.adds + old * g + h + 1)
                        act.wait_ge(scores_ok, t.steps + s + 1)
                        act.activation(probs[:, s % RING, :], scores[s % 2][:, :], ACT.Exp,
                                       scale=(1.0, float(D1) ** 0.5 / QK_SCALE ** 2)[l]).then_inc(exp_ok, 1)
                    for kind, i in chunk(l, kt, not last, not first):
                        unit(kind, i, t.bank, u, side, post)
                        u += 1
                    if l == 1 and not last:
                        highs(kt, side, t.bank, not first)
                act.wait_ge(o_norm_ok, PRIMED + t.turns)
                act.wait_ge(av_ok, t.avs + KT)
                act.activation(o_raw[:, :], o_acc[:, :], ACT.Copy).then_inc(o_copied, 1)

            def evacuate(bank, u, dst, n_c, scale, bias):
                for c in range(n_c):
                    for n in range(NH):
                        act.wait_ge(work_full, 2 * bank + u + 1)
                        if scale is None:
                            a = act.activation(dst[:, c, tokens(n)], work[u % 2][:, :], ACT.Copy)
                        else:
                            a = act.activation(dst[:, c, tokens(n)], work[u % 2][:, :], ACT.Identity,
                                               scale=affine[:, scale, c:c + 1],
                                               bias=0.0 if bias is None else affine[:, bias, c:c + 1])
                        a.then_inc(work_free[u % 2], 1)
                        u += 1
                return u

            act.wait_ge(consts_in, 16 * 7)
            with act.Fori(0, B) as b:
                start = b * (BATCH_UNITS // 2)
                u = evacuate(start, 0, cT, CC, None, None)
                evacuate(start, u, hT, XC, 0, 1)
                run_layer(act, b, 0, unit, one_turn)
                evacuate(side0_start(b, 1) - MID_UNITS // 2, 0, hT, XC, 2, None)
                run_layer(act, b, 1, unit, one_turn, highs)

        @block.vector
        def _(dve):
            def unit(kind, i, bank, u, side, post):
                w = work[u % 2]
                full = 2 * bank + u + 1
                if kind in ("k", "q") and side.layer == 0:
                    dve.wait_ge(work_full, full)
                    dve.wait_ge(high_ok, 4 * side.sides + 2 * (kind == "q") + i + 1)
                    for h in range(G0):
                        hi = (k_parts if kind == "k" else q_high)[side.par][h][0:D0, tokens(i)].bitcast(F32)
                        lo = k_parts[side.par][h][D0:P, tokens(i)] if kind == "k" else q_low[side.par][h][0:D0, tokens(i)]
                        v = dve.tensor_tensor(lo, w[h * D0:(h + 1) * D0, :], hi, ALU.subtract)
                    v.then_inc(work_free[u % 2], 1)
                elif kind == "rowmax":
                    h, qt, n = i // (TT * NH), i // NH % TT, i % NH
                    dve.wait_ge(work_full, full)
                    dve.tensor_reduce(tile_max[:, h, qt, n:n + 1], w[:, :], AX.X, ALU.max, negate=True).then_inc(work_free[u % 2], 1)
                    if i % (TT * NH) == TT * NH - 1:
                        for k in range(2):
                            wait_unit_evacuated(dve, bank, u - k)
                        dve.tensor_reduce(neg_max[:, h, :], tile_max[:, h, :, :], AX.X, ALU.min).then_inc(neg_max_ok, 1)
                elif kind == "den" and i == NH - 1:
                    g = (G0, G1)[post.layer]
                    dve.wait_ge(den_in, 16 * post.turns)
                    dve.reciprocal(recip_t[:, 0:g, :], den_t[:, 0:g, :]).then_inc(recip_ok, 1)
                elif kind == "out":
                    if i == 0:
                        dve.wait_ge(recip_in, 16 * G1 * post.turns)
                        dve.wait_ge(o_copied, PRIMED + post.turns)
                        dve.tensor_tensor(o_norm[:, :], o_raw[:, :], recip[:, :], ALU.mult).then_inc(o_norm_ok, 1)
                        dve.wait_ge(bias_ok, post.b + 1)
                    dve.wait_ge(work_full, full)
                    dve.tensor_tensor(resid[:, i, :], w[:, :], resid[:, i, :], ALU.add).then_inc(work_free[u % 2], 1)

            def norms(kt, side, bank, post):
                n = NORM_STEPS * side.sides
                for which, at in ((0, 2), (1, 3)):
                    if kt == at:
                        m = n + 3 * which
                        vec = raw[which][:, :, :, :].rearrange("p t h d -> p (t h) d")
                        dve.wait_ge(rope_step, ROPE_STEPS * side.sides + 4 * (which + 1))
                        if which == 1:
                            dve.wait_ge(norm_step, n + 2)
                        dve.tensor_tensor(squares[:, :, :], vec, vec, ALU.mult).then_inc(norm_step, 1)
                        dve.wait_ge(norm_step, m + 1)
                        dve.tensor_reduce(sumsq[:, which, :], squares[:, :, :], AX.X, ALU.add).then_inc(norm_step, 1)
                        dve.wait_ge(norm_step, m + 2)
                        dve.tensor_scalar(sumsq[:, which, :], sumsq[:, which, :], L2_EPS ** 2, QK_SCALE ** -2, ALU.max, ALU.mult).then_inc(norm_step, 1)
                for which, at in ((0, 5), (1, 6)):
                    if kt == at:
                        m = n + 6 + 3 * which
                        dve.wait_ge(high1_ok, 2 * side.sides + which + 1)
                        vec = raw[which][:, :, :, :].rearrange("p t h d -> p (t h) d")
                        low = (2, 1)[which]
                        dve.tensor_tensor(stack[which][:, :, low, :], vec, stack[which][:, :, 0, :], ALU.subtract).then_inc(norm_step, 1)
                        dve.tensor_copy(stack[which][:, :, (1, 2)[which], :], stack[which][:, :, 0, :]).then_inc(norm_step, 1)
                        dve.wait_ge(norm_step, m + 1)
                        dve.tensor_copy(stack[which][:, :, 3, :], stack[which][:, :, low, :]).then_inc(norm_step, 1)

            def one_turn(l, b, p, par, first, last, j=None):
                t = Counts(b, l, p)
                side, post = sides_of(b, l, p, par, j)
                g = (G0, G1)[l]
                u = 0
                for kt in range(KT):
                    units = chunk(l, kt, not last, not first)
                    for h in range(g):
                        s = kt * g + h
                        if kt > 0:
                            dve.wait_ge(exp_ok, t.steps + s + 1)
                            if kt > 1:
                                dve.wait_ge(add_ok, t.adds + (kt - 2) * g + h + 1)
                            before = probs[:, s - g, :] if kt == 1 else acc[h][:, :]
                            dve.tensor_tensor(acc[h][:, :], before, probs[:, s % RING, :], ALU.add).then_inc(add_ok, 1)
                        for kind, i in share(units, h, g):
                            unit(kind, i, t.bank, u, side, post)
                            u += 1
                    if l == 1 and not last:
                        norms(kt, side, t.bank, not first)

            def row_norm(l, b):
                n = 2 * b + l
                for t in range(TT):
                    v = dve.bn_stats(stats[:, t, :], resid[:, t, :])
                v.then_inc(bn_ok, 1)
                dve.wait_ge(bn_ok, n + 1)
                dve.memset(gate_v[:, 0:1], 0.0)
                for t in range(TT):
                    v = dve.bn_aggr(mv[:, t, :], stats[:, t, :])
                v.then_inc(aggr_ok, 1)
                dve.wait_ge(aggr_ok, n + 1)
                if l == 0:
                    dve.tensor_scalar(var_eps[:, :], mv[:, :, 1], LN_EPS, None, ALU.add).then_inc(var_ok, 1)
                else:
                    dve.tensor_tensor(mean_sq[:, :], mv[:, :, 0], mv[:, :, 0], ALU.mult).then_inc(mean_sq_step, 1)
                    dve.wait_ge(mean_sq_step, 2 * b + 1)
                    dve.tensor_tensor(mean_sq[:, :], mean_sq[:, :], mv[:, :, 1], ALU.add).then_inc(mean_sq_step, 1)
                    dve.wait_ge(mean_sq_step, 2 * b + 2)
                    dve.tensor_scalar(var_eps[:, :], mean_sq[:, :], RMS_EPS, None, ALU.add).then_inc(var_ok, 1)
                dve.wait_ge(rstd_ok, 2 * b + l + 1)
                for t in range(TT):
                    if l == 0:
                        v = dve.tensor_scalar(xn[:, t, :], resid[:, t, :], mv[:, t, 0:1], rstd[:, t:t + 1], ALU.subtract, ALU.mult)
                    else:
                        v = dve.tensor_scalar(xn[:, t, :], resid[:, t, :], rstd[:, t:t + 1], None, ALU.mult)
                    v.then_inc(xn_ok, 1)

            for n, counter in enumerate((work_free[0], work_free[1], o_copied, o_norm_ok)):
                dve.memset(gate_v[:, 1 + n:2 + n], 0.0).then_inc(counter, PRIMED)
            dve.memset(gate_v[:, 5:6], 0.0).then_inc(stored, 16 * PRIMED)
            dve.memset(ones[0][:, :], float(D0) ** 0.5)
            dve.memset(ones[1][:, :], 1.0)
            dve.wait_ge(consts_in, 16 * 7)
            dve.tensor_copy(ident_r[:, :], ident[:, :])
            dve.tensor_copy(ident_h[:, :], ident[:, :]).then_inc(consts_ok, 1)
            with dve.Fori(0, B) as b:
                dve.wait_ge(x_in, 16 * (b + 1))
                for i in range(2):
                    for h in range(G0):
                        dve.memset(k_one[i][h][D0:D0 + 1, :].bitcast(F32), 1.0)
                row_norm(0, b)
                run_layer(dve, b, 0, unit, one_turn)
                wait_all_evacuated(dve, side0_start(b, 1) - MID_UNITS // 2)
                row_norm(1, b)
                run_layer(dve, b, 1, unit, one_turn, norms)

        @block.gpsimd
        def _(pool):
            def unit(kind, i, bank, u, side, post):
                if kind == "k" and side.layer == 0:
                    pool.wait_ge(high_ok, 4 * side.sides + i + 1)
                    pool.tensor_tensor(gate_p[:, i:i + 1], power[:, 0:1], power[:, 0:1], ALU.mult)
                    for h in range(G0):
                        c = pool.tensor_copy(k_one[side.par][h][0:D0, tokens(i)], k_parts[side.par][h][0:D0, tokens(i)].bitcast(F32))
                    c.then_inc(dup_ok, 1)

            def rope(which, side, bank, u):
                n = ROPE_STEPS * side.sides + 4 * which
                wait_unit_evacuated(pool, bank, u - 2)
                wait_unit_evacuated(pool, bank, u - 1)
                r, half = raw[which], D1 // 2
                c4 = cos[:, :, :].unsqueeze(2).broadcast_to([P, TT, G1, D1])
                s4 = sin[:, :, :].unsqueeze(2).broadcast_to([P, TT, G1, D1])
                if which == 1:
                    pool.wait_ge(rope_step, n)
                pool.tensor_tensor(rot[:, :, :, :], r[:, :, :, :], c4, ALU.mult).then_inc(rope_step, 1)
                pool.tensor_tensor(tmp[:, :, :, 0:half], r[:, :, :, half:D1], s4[:, :, :, 0:half], ALU.mult).then_inc(rope_step, 1)
                pool.tensor_tensor(tmp[:, :, :, half:D1], r[:, :, :, 0:half], s4[:, :, :, half:D1], ALU.mult).then_inc(rope_step, 1)
                pool.wait_ge(rope_step, n + 3)
                pool.tensor_tensor(r[:, :, :, :], rot[:, :, :, :], tmp[:, :, :, :], ALU.add).then_inc(rope_step, 1)

            def scale(which, side):
                n = ROPE_STEPS * side.sides + 8 + 2 * which
                vec = raw[which][:, :, :, :].rearrange("p t h d -> p (t h) d")
                pool.wait_ge(norm_step, NORM_STEPS * side.sides + 3 * (which + 1))
                pool.tensor_tensor(inv[:, which, :], sumsq[:, which, :], power[:, :], ALU.pow).then_inc(rope_step, 1)
                pool.wait_ge(rope_step, n + 1)
                pool.tensor_tensor(vec, vec, inv[:, which, :].unsqueeze(2).broadcast_to([P, TT * G1, D1]), ALU.mult).then_inc(rope_step, 1)

            def rotations(kt, side, bank, post):
                ends = [sum(len(chunk(1, c, True, post)) for c in range(n + 1)) for n in range(2)]
                if kt == 1:
                    rope(0, side, bank, ends[0])
                    rope(1, side, bank, ends[1])
                    scale(0, side)
                    scale(1, side)

            def one_turn(l, b, p, par, first, last, j=None):
                t = Counts(b, l, p)
                side, post = sides_of(b, l, p, par, j)
                u = 0
                for kt in range(0 if last else KT):
                    for kind, i in chunk(l, kt, True, not first):
                        unit(kind, i, t.bank, u, side, post)
                        u += 1
                    if l == 1:
                        rotations(kt, side, t.bank, not first)

            def row_power(n):
                pool.wait_ge(var_ok, n + 1)
                pool.tensor_tensor(rstd[:, :], var_eps[:, :], power[:, 0:TT], ALU.pow).then_inc(rstd_ok, 1)

            pool.memset(power[:, :], -0.5).then_inc(power_ok, 1)
            pool.wait_ge(power_ok, 1)
            pool.wait_ge(consts_in, 16 * 7)
            with pool.Fori(0, B) as b:
                row_power(2 * b)
                pool.wait_ge(xn_ok, 2 * TT * b + TT)
                pool.tensor_tensor(resid[:, :, :], resid[:, :, :], bo_all[:, :].unsqueeze(1).broadcast_to([P, TT, D]), ALU.add).then_inc(bias_ok, 1)
                run_layer(pool, b, 0, unit, one_turn)
                row_power(2 * b + 1)
                run_layer(pool, b, 1, unit, one_turn, rotations)


_INS = ['x', 'ctx_768', 'L0_xattn_Wq', 'L0_xattn_Wk', 'L0_xattn_Wv', 'L0_xattn_Wo', 'L0_xattn_bo', 'L0_xattn_gamma',
        'L0_xattn_beta', 'L1_xattn_norm_w', 'L1_xattn_wq', 'L1_xattn_wkv', 'L1_xattn_wout']
_OUTS = [((B, S, D), 'float32')]


def rope_tables():
    inv_freq = 1.0 / 10000.0 ** (np.arange(0, D1, 2, dtype=np.float32) / D1)
    freqs = np.einsum('i,j->ij', np.arange(S, dtype=np.float32), inv_freq)
    emb = np.concatenate([freqs, freqs], axis=-1)
    sign = np.where(np.arange(D1) < D1 // 2, -1.0, 1.0)
    return np.cos(emb).astype(np.float32), (np.sin(emb) * sign).astype(np.float32)


def kernel(**inputs):
    import numpy as _np
    import concourse.bacc as _bacc
    from concourse import mybir as _mybir
    from concourse.bass_utils import run_bass_kernel_spmd as _run

    nc = _bacc.Bacc("TRN2", target_bir_lowering=False, num_devices=1)
    arrays, args = {}, []
    given = {name: _np.ascontiguousarray(inputs[name]) for name in _INS}
    given["cos"], given["sin"] = rope_tables()
    given["ident"] = _np.eye(P, dtype=_np.float32)
    for name, a in given.items():
        arrays[f"in_{name}_dram"] = a
        args.append(nc.dram_tensor(f"in_{name}_dram", a.shape, _mybir.dt.from_np(a.dtype), kind="ExternalInput").ap())
    for i, (shape, dtype) in enumerate(_OUTS):
        dt = _mybir.dt.from_np(_np.dtype(dtype))
        args.append(nc.dram_tensor(f"out_{i}_dram", shape, dt, kind="ExternalOutput").ap())
    rows = nc.dram_tensor("rows_dram", (2, G1, S), _mybir.dt.float32, kind="Internal").ap()
    build(nc, rows, *args)
    r = _run(nc, [arrays], core_ids=[0])
    got = tuple(r.results[0][f"out_{i}_dram"] for i in range(len(_OUTS)))
    return got[0]
```

```python
from contextlib import ExitStack

import numpy as np

import concourse.bass as bass
from concourse import mybir

F32 = mybir.dt.float32
F32R = mybir.dt.float32r
F16 = mybir.dt.float16
ALU = mybir.AluOpType
ACT = mybir.ActivationFunctionType
AX = mybir.AxisListType

B, S, D, DC = 4, 1024, 512, 384
P = 128
TT = S // P
NH = S // 512
XC, CC = D // P, DC // P
HEADS = 16
D0, D1 = 64, D // HEADS
G0, G1 = P // D0, P // D1
TURNS0, TURNS1 = HEADS // G0, HEADS // G1
KT = S // P
LN_EPS = RMS_EPS = 1e-5
L2_EPS = 1e-12
QK_SCALE = 64.0
PRIMED = 1
RING = 8


class Turn:

    def __init__(self, owner):
        self.owner = owner

    def __call__(self, kind, a, b=None):
        return [(kind, i, self.owner) for i in range(a, a + 1 if b is None else b)]


post, nxt, ahead = Turn("post"), Turn("next"), Turn("ahead")
UNITS = (
    [nxt("q", 0, 2) + post("den", 0, 2),
     nxt("rowmax", 0, 3) + nxt("v", 0) + nxt("rowmax", 3, 6),
     nxt("rowmax", 6, 9) + nxt("v", 1) + nxt("rowmax", 9, 12),
     nxt("rowmax", 12, 15) + post("out", 0) + nxt("rowmax", 15) + post("out", 1),
     nxt("rowmax", 16) + post("out", 2) + nxt("rowmax", 17) + nxt("shift", 0) + nxt("rowmax", 18) + post("out", 3)
     + nxt("shift", 1) + nxt("rowmax", 19, 22),
     nxt("rowmax", 22) + post("out", 4) + nxt("rowmax", 23, 25) + post("out", 5) + nxt("rowmax", 25, 27),
     nxt("rowmax", 27) + post("out", 6) + nxt("rowmax", 28, 30) + post("out", 7) + nxt("rowmax", 30, 32),
     nxt("shift", 2, 4) + ahead("k", 0, 2)],
    [post("den", 0, 2),
     nxt("v", 0),
     nxt("v", 1),
     post("out", 0, 2),
     post("out", 2, 4),
     post("out", 4, 6) + nxt("turn_k", 0, G1),
     post("out", 6, 8) + nxt("turn_q", 0, G1) + ahead("k", 0, 2),
     ahead("q", 0, 2)])
RECIP_AT = 2


def chunk(layer, kt, nxt, ahead, post):
    there = {"post": post, "next": nxt, "ahead": ahead}
    return [w for w in UNITS[layer][kt] if there[w[2]]]


def opening(layer, step):
    if layer == 1:
        return (nxt("k", 0, 2) + nxt("q", 0, 2) if step == 0 else []) + chunk(1, step, True, True, False)
    return [nxt("k", 0, 2) + nxt("q", 0, 2),
            nxt("rowmax", 0, 8) + nxt("v", 0),
            nxt("rowmax", 8, 16) + nxt("v", 1),
            nxt("shift", 0, 2) + nxt("rowmax", 16, 20),
            nxt("rowmax", 20, 24) + ahead("k", 0),
            nxt("rowmax", 24, 28) + ahead("k", 1),
            nxt("rowmax", 28, 32),
            nxt("shift", 2, 4)][step]


def share(items, part, parts):
    return items[part * len(items) // parts:(part + 1) * len(items) // parts]


def n_units(layer, nxt, ahead, post):
    return sum(len(chunk(layer, kt, nxt, ahead, post)) for kt in range(KT))


PREP_UNITS = (CC + XC) * NH
MID_UNITS = XC * NH
TURNS = (TURNS0, TURNS1)
STEPS = (KT * G0, KT * G1)
ADDS = ((KT - 1) * G0, (KT - 1) * G1)
OPENING = tuple(sum(len(opening(l, s)) for s in range(KT)) for l in (0, 1))
FIRST = tuple(n_units(l, True, True, False) for l in (0, 1))
BODY = tuple(n_units(l, True, True, True) for l in (0, 1))
LAST = n_units(0, False, False, True)
N_AHEAD = tuple(sum(w[2] == "ahead" for units in UNITS[l] for w in units) for l in (0, 1))
N_Q = len(nxt("q", 0, 2))


def layer_units(l):
    return OPENING[l] + FIRST[l] + (TURNS[l] - 2) * BODY[l] - N_AHEAD[l] + 2 * LAST


BATCH_UNITS = PREP_UNITS + layer_units(0) + MID_UNITS + layer_units(1)
TURNS_B = sum(TURNS)


def layer_start(b, l):
    return b * (BATCH_UNITS // 2) + (PREP_UNITS + l * (layer_units(0) + MID_UNITS)) // 2


class Counts:

    def __init__(self, b, l, p):
        self.bank = layer_start(b, l) + OPENING[l] // 2
        if not (isinstance(p, int) and p == 0):
            self.bank = self.bank + FIRST[l] // 2 + (p - 1) * (BODY[l] // 2)
        if isinstance(p, int) and p >= TURNS[l] - 1:
            self.bank = self.bank - N_AHEAD[l] // 2 - (p - TURNS[l] + 1) * (BODY[l] - LAST) // 2
        self.turns = b * TURNS_B + l * TURNS0 + p
        self.avs = self.turns * KT
        self.steps = (b * (TURNS0 * STEPS[0] + TURNS1 * STEPS[1]) + l * TURNS0 * STEPS[0]
                      + p * STEPS[l])
        self.adds = (b * (TURNS0 * ADDS[0] + TURNS1 * ADDS[1]) + l * TURNS0 * ADDS[0]
                     + p * ADDS[l])
        self.sides = b * TURNS[l] + p


class Share:

    def __init__(self, b, layer, par, turns, adds, sides, w_count, opening=False):
        self.b, self.layer, self.par = b, layer, par
        self.opening = opening
        self.turns, self.adds, self.sides, self.w_count = turns, adds, sides, w_count


def build(nc, rows, x, ctx_in, wq0, wk0, wv0, wo0, bo, gamma, beta, norm_w, wq1, wkv1, wout1,
          cos_t, sin_t, ident_t, out):
    W0 = {"q": wq0.rearrange("(c p) n -> p c n", p=P), "k": wk0.rearrange("(c p) n -> p c n", p=P),
          "v": wv0.rearrange("(c p) n -> p c n", p=P), "o": wo0}
    kv1 = wkv1.rearrange("(c p) n -> p c n", p=P)
    W1 = {"q": wq1.rearrange("(c p) n -> p c n", p=P), "k": kv1[:, :, 0:D], "v": kv1[:, :, D:2 * D],
          "o": wout1}
    WEIGHTS = (W0, W1)
    x_rows = x.rearrange("b (t p) d -> b p t d", p=P)
    c_rows = ctx_in.rearrange("b (t p) d -> b p t d", p=P)
    out_rows = out.rearrange("b (t p) d -> b p t d", p=P)

    with ExitStack() as ctx:
        def sb(name, shape, dt=F32, scope=ctx):
            return scope.enter_context(nc.sbuf_tensor(name, shape, dt))

        def sem(name):
            return ctx.enter_context(nc.semaphore(name))

        ident = sb("ident", [P, P])
        ident_r = sb("ident_r", [P, P], F32R)
        ident_h = sb("ident_h", [P, P], F16)
        ones = [sb("ones_scaled", [P, D0]), sb("ones_plain", [P, D0])]
        cos = sb("cos", [P, TT, D1])
        sin = sb("sin", [P, TT, D1])
        affine = sb("affine", [P, 3, XC])
        bo_all = sb("bo_all", [P, D])
        stats = sb("stats", [P, TT, 6])
        mv = sb("mv", [P, TT, 2])
        var_eps = sb("var_eps", [P, TT])
        mean_sq = sb("mean_sq", [P, TT])
        rstd = sb("rstd", [P, TT])
        gate_v = sb("gate_v", [P, 6])
        gate_p = sb("gate_p", [P, 2 * NH])
        power = sb("power", [P, TT * G1])
        resid = sb("resid", [P, TT, D])
        hT = sb("hT", [P, XC, S])
        cT = sb("cT", [P, CC, S])
        wq = [sb(f"wq{i}", [P, XC, P]) for i in range(2)]
        wk = [sb(f"wk{i}", [P, CC, P]) for i in range(2)]
        wv = [sb(f"wv{i}", [P, CC, P]) for i in range(2)]
        wo = [sb(f"wo{i}", [P, D]) for i in range(2)]
        v_tok = [sb(f"v_tok{i}", [P, KT, P]) for i in range(2)]
        probs = sb("probs", [P, RING, S])
        acc = [sb(f"acc{h}", [P, S]) for h in range(G1)]
        o_raw = sb("o_raw", [P, S])
        recip = sb("recip", [P, S])
        den_t = sb("den_t", [P, G1, TT])
        recip_t = sb("recip_t", [P, G1, TT])
        o_norm = sb("o_norm", [P, S])
        xn = probs[:, 0:4, :].rearrange("p a b -> p (a b)").rearrange("p (t d) -> p t d", d=D)
        c_raw = probs[:, 4:7, :].rearrange("p a b -> p (a b)").rearrange("p (t d) -> p t d", d=DC)

        with ExitStack() as scope:
            k_parts = [[sb(f"k_parts{i}{h}", [P, S], F32R, scope) for h in range(G0)] for i in range(2)]
            k_one = [[sb(f"k_one{i}{h}", [D0 + 1, S], F32R, scope) for h in range(G0)] for i in range(2)]
            q_high = [[sb(f"q_high{i}{h}", [P, S], F32R, scope) for h in range(G0)] for i in range(2)]
            q_low = [[sb(f"q_low{i}{h}", [D0 + 1, S], F32R, scope) for h in range(G0)] for i in range(2)]
            tile_max = sb("tile_max", [P, G0, TT, NH], F32, scope)
            neg_max = sb("neg_max", [P, G0, TT], F32R, scope)
        with ExitStack() as scope:
            kT = [sb(f"kT{i}", [P, G1, S], F16, scope) for i in range(2)]
            qT = [sb(f"qT{i}", [P, G1, S], F16, scope) for i in range(2)]
            stack = [sb(f"stack{n}", [P, TT * G1, 4, D1], F16, scope) for n in ("k", "q")]
            raw = [sb(f"raw{n}", [P, TT, G1, D1], F32, scope) for n in ("k", "q")]
            rot = sb("rot", [P, TT, G1, D1], F32, scope)
            tmp = sb("tmp", [P, TT, G1, D1], F32, scope)
            squares = sb("squares", [P, TT * G1, D1], F32, scope)
            sumsq = sb("sumsq", [P, 2, TT * G1], F32, scope)
            inv = sb("inv", [P, 2, TT * G1], F32, scope)

        scores = [ctx.enter_context(nc.psum_tensor(f"scores{i}", [P, S], F32)) for i in range(2)]
        o_acc = ctx.enter_context(nc.psum_tensor("o_acc", [P, S], F32))
        work = [ctx.enter_context(nc.psum_tensor(f"work{i}", [P, 512], F32)) for i in range(2)]
        work_h = [w[:, :].bitcast(F16) for w in work]

        consts_in = sem("consts_in")
        consts_ok = sem("consts_ok")
        x_in = sem("x_in")
        c_in = sem("c_in")
        w_in = [sem(f"w_in{i}") for i in range(2)]
        wo_in = [sem(f"wo_in{i}") for i in range(2)]
        stored = sem("stored")
        bn_ok = sem("bn_ok")
        aggr_ok = sem("aggr_ok")
        mean_sq_step = sem("mean_sq_step")
        var_ok = sem("var_ok")
        rstd_ok = sem("rstd_ok")
        xn_ok = sem("xn_ok")
        bias_ok = sem("bias_ok")
        power_ok = sem("power_ok")
        work_full = sem("work_full")
        work_free = [sem(f"work_free{i}") for i in range(2)]
        high_ok = sem("high_ok")
        dup_ok = sem("dup_ok")
        neg_max_ok = sem("neg_max_ok")
        scores_ok = sem("scores_ok")
        exp_ok = sem("exp_ok")
        add_ok = sem("add_ok")
        av_ok = sem("av_ok")
        o_copied = sem("o_copied")
        o_norm_ok = sem("o_norm_ok")
        den_out = sem("den_out")
        den_in = sem("den_in")
        recip_ok = sem("recip_ok")
        recip_out = sem("recip_out")
        recip_in = sem("recip_in")
        high1_ok = sem("high1_ok")
        rope_step = sem("rope_step")
        norm_step = sem("norm_step")
        ROPE_STEPS, NORM_STEPS = 12, 12
        def shares(b, l, p, par, j=None, opening=False):
            t = Counts(b, l, p)
            if j is None:
                half = {"post": (p - 1) // 2, "next": (p + 1) // 2, "ahead": p // 2 + 1}
            else:
                half = {"post": j, "next": j + 1, "ahead": j + 2 - par}
            loads = {k: b * (TURNS_B // 2) + l * (TURNS0 // 2) + v + 1 for k, v in half.items()}
            return {"post": Share(b, l, 1 - par, t.turns, t.adds, None, 16 * loads["post"]),
                    "next": Share(b, l, 1 - par, None, None, t.sides + 1, 48 * loads["next"], opening),
                    "ahead": Share(b, l, par, None, None, t.sides + 2, 48 * loads["ahead"])}

        def first_den(l, nxt):
            return N_Q if l == 0 and nxt else 0

        def run_layer(eng, b, l, unit, one_turn, chain=None, behind=None):
            who = shares(b, l, -1, 1, None, True)
            start = layer_start(b, l)
            u = 0
            for step in range(KT):
                for kind, i, w in opening(l, step):
                    unit(kind, i, start, u, who[w])
                    u += 1
                if chain is not None and l == 1:
                    chain(step, who["next"], start, 2 * N_Q)
            one_turn(l, b, 0, 0)
            if l == 0:
                with eng.Fori(0, (TURNS0 - 4) // 2) as j:
                    for i in range(2):
                        one_turn(l, b, 2 * j + 1 + i, 1 - i, j)
            for p in range(TURNS0 - 3 if l == 0 else 1, TURNS[l]):
                one_turn(l, b, p, p % 2)
            post = shares(b, l, TURNS[l], 0)["post"]
            u = 0
            for kt in range(KT):
                if behind is not None:
                    behind(kt, post)
                for kind, i, _ in chunk(l, kt, False, False, True):
                    unit(kind, i, Counts(b, l, TURNS[l]).bank, u, post)
                    u += 1

        def has(l, p, j):
            if j is not None:
                return True, True, True
            return p < TURNS[l] - 1, p < TURNS[l] - 2, p > 0

        block = ctx.enter_context(nc.Block())

        def wait_unit_evacuated(eng, bank, u):
            eng.wait_ge(work_free[u % 2], PRIMED + bank + (u // 2 + 1))

        def wait_all_evacuated(eng, bank):
            for i in range(2):
                eng.wait_ge(work_free[i], PRIMED + bank)

        def tokens(n):
            return slice(n * 512, (n + 1) * 512)

        def tile(t):
            return slice(t * P, (t + 1) * P)

        @block.sync
        def _(sp):
            for dst, src in ((ident[:, :], ident_t), (cos[:, :, :], cos_t.rearrange("(t p) d -> p t d", p=P)),
                             (sin[:, :, :], sin_t.rearrange("(t p) d -> p t d", p=P)),
                             (affine[:, 0, :], gamma.rearrange("(c p) -> p c", p=P)),
                             (affine[:, 1, :], beta.rearrange("(c p) -> p c", p=P)),
                             (affine[:, 2, :], norm_w.rearrange("(c p) -> p c", p=P)),
                             (bo_all[:, :], bo.rearrange("(a n) -> a n", a=1).to_broadcast([P, D]))):
                with nc.allow_non_contiguous_dma("small constants, once"):
                    sp.dma_start(dst, src).then_inc(consts_in, 16)

            def load_side(l, p, par):
                for name, dst in (("q", wq), ("k", wk), ("v", wv)):
                    sp.dma_start(dst[par][:, :, :], WEIGHTS[l][name][:, :, bass.ds(p * P, P)]).then_inc(w_in[par], 16)

            def load_out(l, p, par):
                sp.dma_start(wo[par][:, :], WEIGHTS[l]["o"][bass.ds(p * P, P), :]).then_inc(wo_in[par], 16)

            def after(b, l, p):
                sp.wait_ge(work_full, 2 * Counts(b, l, p).bank)

            def turn_sums(b, l, bank, turns, first):
                g, d = ((G0, D0), (G1, D1))[l]
                wait_unit_evacuated(sp, bank, first)
                wait_unit_evacuated(sp, bank, first + 1)
                sp.dma_start(rows[0, 0:g, :], recip[0:(g - 1) * d + 1:d, :]).then_inc(den_out, 16)
                with nc.allow_non_contiguous_dma("runs of eight sums"):
                    sp.wait_ge(den_out, 16 * turns)
                    sp.dma_start(den_t[:, 0:g, :], rows[0, 0:g, :].rearrange("h (p j) -> p h j", j=TT)).then_inc(den_in, 16)
                    sp.wait_ge(recip_ok, turns)
                    sp.dma_start(rows[1, 0:g, :].rearrange("h (p j) -> p h j", j=TT), recip_t[:, 0:g, :]).then_inc(recip_out, 16)
                sp.wait_ge(recip_out, 16 * turns)
                for h in range(G1):
                    row = h * g // G1
                    sp.dma_start(recip[h * D1:(h + 1) * D1, :], rows[1, row:row + 1, :].to_broadcast([D1, S])).then_inc(recip_in, 16)

            load_side(0, 0, 0)
            load_side(0, 1, 1)
            with sp.Fori(0, B) as b:
                sp.wait_ge(stored, 16 * (PRIMED + b))
                sp.dma_start(c_raw, c_rows[bass.ds(b, 1), :, :, :].rearrange("a p t d -> p (a t) d")).then_inc(c_in, 16)
                sp.dma_start(resid[:, :, :], x_rows[bass.ds(b, 1), :, :, :].rearrange("a p t d -> p (a t) d")).then_inc(x_in, 16)
                after(b, 0, 0)
                load_out(0, 0, 0)
                load_side(0, 2, 0)
                with sp.Fori(0, (TURNS0 - 4) // 2) as j:
                    for i in range(2):
                        p = 2 * j + 1 + i
                        after(b, 0, p)
                        load_out(0, p, 1 - i)
                        load_side(0, p + 2, 1 - i)
                        turn_sums(b, 0, Counts(b, 0, p).bank, Counts(b, 0, p).turns, first_den(0, True))
                after(b, 0, TURNS0 - 3)
                load_out(0, TURNS0 - 3, 1)
                load_side(0, TURNS0 - 1, 1)
                turn_sums(b, 0, Counts(b, 0, TURNS0 - 3).bank, Counts(b, 0, TURNS0 - 3).turns, first_den(0, True))
                for p in (TURNS0 - 2, TURNS0 - 1):
                    after(b, 0, p)
                    load_out(0, p, p % 2)
                    load_side(1, p - (TURNS0 - 2), p % 2)
                    turn_sums(b, 0, Counts(b, 0, p).bank, Counts(b, 0, p).turns, first_den(0, p < TURNS0 - 1))
                turn_sums(b, 0, Counts(b, 0, TURNS0 - 1).bank + LAST // 2, Counts(b, 0, TURNS0).turns, 0)
                for p in range(TURNS1):
                    after(b, 1, p)
                    load_out(1, p, p % 2)
                    if p < TURNS1 - 2:
                        load_side(1, p + 2, p % 2)
                    else:
                        load_side(0, p - (TURNS1 - 2), p % 2)
                    if p > 0:
                        turn_sums(b, 1, Counts(b, 1, p).bank, Counts(b, 1, p).turns, 0)
                turn_sums(b, 1, Counts(b, 1, TURNS1 - 1).bank + LAST // 2, Counts(b, 1, TURNS1).turns, 0)
                wait_all_evacuated(sp, (b + 1) * (BATCH_UNITS // 2))
                sp.dma_start(out_rows[bass.ds(b, 1), :, :, :].rearrange("a p t d -> p (a t) d"), resid[:, :, :]).then_inc(stored, 16)
            sp.wait_ge(stored, 16 * (PRIMED + B))
            for i in range(2):
                sp.wait_ge(w_in[i], 48 * (B * TURNS_B // 2 + 1))

        @block.tensor
        def _(pe):
            def unit(kind, i, bank, u, who):
                w = work[u % 2]
                pe.wait_ge(work_free[u % 2], PRIMED + bank + u // 2)
                if kind in ("k", "q", "v"):
                    par = who.par
                    if kind == "k" and i == 0:
                        pe.wait_ge(w_in[par], who.w_count)
                    wt = {"k": wk, "q": wq, "v": wv}[kind][par]
                    src, n_c = (hT, XC) if kind == "q" else (cT, CC)
                    if who.layer == 0 and kind != "v":
                        for c in range(n_c):
                            mm = pe.matmul(w[:, :], wt[:, c, :], src[:, c, tokens(i)], start=(c == 0), stop=(c == n_c - 1))
                    else:
                        for t in range(4):
                            for c in range(n_c):
                                mm = pe.matmul(w[:, tile(t)], src[:, c, tile(4 * i + t)], wt[:, c, :], start=(c == 0), stop=(c == n_c - 1))
                elif kind == "rowmax":
                    if i == 0:
                        wait_unit_evacuated(pe, bank, 2 * N_Q - 1 if who.opening else N_Q - 1)
                    h, qt, n = i // (TT * NH), i // NH % TT, i % NH
                    mm = pe.matmul(w[:, :], q_high[who.par][h][:, tile(qt)], k_parts[who.par][h][:, tokens(n)], start=True, stop=True)
                elif kind == "shift":
                    h, n = i // NH, i % NH
                    if n == 0:
                        pe.wait_ge(neg_max_ok, G0 * who.sides + h + 1)
                    for t in range(4):
                        qt = 4 * n + t
                        mm = pe.matmul(w[0:1, tile(t)], neg_max[:, h, qt:qt + 1], ident_r[:, :], start=True, stop=True)
                elif kind in ("turn_k", "turn_q"):
                    which = ("turn_k", "turn_q").index(kind)
                    if i == 0:
                        pe.wait_ge(norm_step, NORM_STEPS * who.sides + (9, 12)[which])
                    for t in range(TT):
                        mm = pe.transpose(work_h[u % 2][:, tile(t)], stack[which][:, t * G1 + i, :, :].rearrange("p a d -> p (a d)"), ident_h[:, :])
                elif kind == "den":
                    if i == 0:
                        pe.wait_ge(add_ok, who.adds)
                    g, d = ((G0, D0), (G1, D1))[who.layer]
                    for h in range(g):
                        mm = pe.matmul(w[h * d:(h + 1) * d, :], ones[who.layer][:, 0:d], acc[h][:, tokens(i)], start=True, stop=True)
                elif kind == "out":
                    if i == 0:
                        pe.wait_ge(o_norm_ok, PRIMED + who.turns)
                        pe.wait_ge(wo_in[who.par], who.w_count)
                    mm = pe.matmul(w[:, :], o_norm[:, tile(i)], wo[who.par][:, :], start=True, stop=True)
                mm.then_inc(work_full, 1)

            def score(l, t, par, kt, h, first):
                s = kt * (G0, G1)[l] + h
                kt = kt % KT
                if not (first and s < 2):
                    pe.wait_ge(exp_ok, t.steps + s - 1)
                for n in range(NH):
                    o = scores[s % 2][:, tokens(n)]
                    if l == 0:
                        pe.matmul(o, k_parts[par][h][:, tile(kt)], q_high[par][h][:, tokens(n)], start=True, stop=False)
                        mm = pe.matmul(o, k_one[par][h][:, tile(kt)], q_low[par][h][:, tokens(n)], start=False, stop=True)
                    else:
                        mm = pe.matmul(o, kT[par][:, h, tile(kt)], qT[par][:, h, tokens(n)], start=True, stop=True)
                mm.then_inc(scores_ok, 1)

            def attend(l, t, par, kt, n):
                g, d = ((G0, D0), (G1, D1))[l]
                if n == 0:
                    pe.wait_ge(exp_ok, t.steps + (kt + 1) * g)
                    if kt == 0:
                        pe.wait_ge(o_copied, PRIMED + t.turns)
                for h in range(g):
                    mm = pe.matmul(o_acc[h * d:(h + 1) * d, tokens(n)], v_tok[par][:, kt, h * d:(h + 1) * d],
                                   probs[:, (kt * g + h) % RING, tokens(n)], start=(kt == 0), stop=(kt == KT - 1))
                if n == NH - 1:
                    mm.then_inc(av_ok, 1)

            def one_turn(l, b, p, par, j=None):
                t = Counts(b, l, p)
                who = shares(b, l, p, par, j)
                nxt, ahead, post = has(l, p, j)
                g = (G0, G1)[l]
                if not post:
                    wait_all_evacuated(pe, t.bank)
                    if l == 0:
                        pe.wait_ge(dup_ok, NH * (t.sides + 1))
                    for h in range(g):
                        score(l, t, par, 0, h, True)
                u = 0
                for kt in range(KT):
                    units = chunk(l, kt, nxt, ahead, post)
                    if l == 0:
                        pieces = [("score", 0), ("score", 1), ("attend", 0), ("attend", 1)]
                        if kt == KT - 1:
                            pieces = [("score", 0), ("attend", 0), ("attend", 1), ("score", 1)]
                        slots = range(kt == KT - 1, len(pieces))
                    else:
                        pieces = [("score", 0), ("score", 1), ("attend", 0), ("score", 2), ("attend", 1), ("score", 3)]
                        slots = range(3)
                    for n, (piece, which) in enumerate(pieces):
                        for kind, i, w in share(units, n - slots.start, len(slots)) if n in slots else []:
                            unit(kind, i, t.bank, u, who[w])
                            if (kind, i) in (("shift", G0 * NH - 1), ("turn_q", G1 - 1)):
                                last_operand = u
                            u += 1
                        if piece == "attend":
                            attend(l, t, par, kt, which)
                        elif kt < KT - 1:
                            score(l, t, par, kt + 1, which, False)
                        elif nxt:
                            if l == 0 and which == 0:
                                pe.wait_ge(dup_ok, NH * (t.sides + 2))
                            elif which == l ^ 1:
                                wait_unit_evacuated(pe, t.bank, last_operand)
                            score(l, t, 1 - par, KT, which, False)

            def transposes(bank, u, src, n_c, ready):
                for c in range(n_c):
                    for n in range(NH):
                        pe.wait_ge(work_free[u % 2], PRIMED + bank + u // 2)
                        if ready is not None and c == 0:
                            pe.wait_ge(xn_ok, ready + 4 * (n + 1))
                        for t in range(4):
                            mm = pe.transpose(work[u % 2][:, tile(t)], src[:, 4 * n + t, tile(c)], ident[:, :])
                        mm.then_inc(work_full, 1)
                        u += 1
                return u

            pe.wait_ge(consts_in, 16 * 7)
            pe.wait_ge(consts_ok, 1)
            with pe.Fori(0, B) as b:
                start = b * (BATCH_UNITS // 2)
                pe.wait_ge(c_in, 16 * (b + 1))
                u = transposes(start, 0, c_raw, CC, None)
                transposes(start, u, xn, XC, 2 * TT * b)
                run_layer(pe, b, 0, unit, one_turn)
                transposes(layer_start(b, 1) - MID_UNITS // 2, 0, xn, XC, 2 * TT * b + TT)
                run_layer(pe, b, 1, unit, one_turn)

        @block.scalar
        def _(act):
            def unit(kind, i, bank, u, who):
                w = work[u % 2]
                full = 2 * bank + u + 1
                if kind in ("k", "q") and who.layer == 0:
                    act.wait_ge(work_full, full)
                    for h in range(G0):
                        dst = (k_parts if kind == "k" else q_high)[who.par][h]
                        a = act.activation(dst[0:D0, tokens(i)], w[h * D0:(h + 1) * D0, :], ACT.Copy)
                        if kind == "q":
                            a = act.activation(dst[D0:P, tokens(i)], w[h * D0:(h + 1) * D0, :], ACT.Copy)
                    a.then_inc(high_ok, 1)
                elif kind in ("k", "q"):
                    act.wait_ge(work_full, full)
                    act.activation(raw[kind == "q"][:, 4 * i:4 * i + 4, :, :].rearrange("p t h d -> p (t h d)"), w[:, :], ACT.Copy).then_inc(work_free[u % 2], 1)
                elif kind == "v":
                    act.wait_ge(work_full, full)
                    act.activation(v_tok[who.par][:, 4 * i:4 * i + 4, :].rearrange("p t d -> p (t d)"), w[:, :], ACT.Copy).then_inc(work_free[u % 2], 1)
                elif kind == "shift":
                    h, n = i // NH, i % NH
                    act.wait_ge(work_full, full)
                    act.activation(q_low[who.par][h][D0:D0 + 1, tokens(n)], w[0:1, :], ACT.Copy).then_inc(work_free[u % 2], 1)
                elif kind in ("turn_k", "turn_q"):
                    act.wait_ge(work_full, full)
                    dst = kT if kind == "turn_k" else qT
                    act.activation(dst[who.par][:, i, :], work_h[u % 2], ACT.Copy).then_inc(work_free[u % 2], 1)
                elif kind == "den":
                    if i == 0:
                        act.wait_ge(o_norm_ok, PRIMED + who.turns - 1)
                    act.wait_ge(work_full, full)
                    act.activation(recip[:, tokens(i)], w[:, :], ACT.Copy).then_inc(work_free[u % 2], 1)

            def highs(kt, who, *_):
                for which, at in ((0, 3), (1, 4)):
                    if kt == at:
                        act.wait_ge(rope_step, ROPE_STEPS * who.sides + (10, 12)[which])
                        act.activation(stack[which][:, :, 0, :], raw[which][:, :, :, :].rearrange("p t h d -> p (t h) d"), ACT.Copy).then_inc(high1_ok, 1)

            def one_turn(l, b, p, par, j=None):
                t = Counts(b, l, p)
                who = shares(b, l, p, par, j)
                nxt, ahead, post = has(l, p, j)
                g = (G0, G1)[l]
                back = RING // g
                u = 0
                for kt in range(KT):
                    for h in range(g):
                        s = kt * g + h
                        old = kt - back
                        if old >= 0:
                            act.wait_ge(av_ok, t.avs + old + 1)
                            act.wait_ge(add_ok, t.adds + (max(old, 1) - 1) * g + h + 1)
                        elif post:
                            act.wait_ge(av_ok, t.avs + old + 1)
                            act.wait_ge(add_ok, t.adds + old * g + h + 1)
                        act.wait_ge(scores_ok, t.steps + s + 1)
                        act.activation(probs[:, s % RING, :], scores[s % 2][:, :], ACT.Exp,
                                       scale=(1.0, float(D1) ** 0.5 / QK_SCALE ** 2)[l]).then_inc(exp_ok, 1)
                    if kt == 0 and post:
                        copy_sums(t.turns, t.avs)
                    for kind, i, w in chunk(l, kt, nxt, ahead, post):
                        unit(kind, i, t.bank, u, who[w])
                        u += 1
                    if l == 1 and nxt:
                        highs(kt, who["next"])
                if not nxt:
                    copy_sums(t.turns + 1, t.avs + KT)

            def copy_sums(turns, avs):
                act.wait_ge(o_norm_ok, PRIMED + turns - 1)
                act.wait_ge(av_ok, avs)
                act.activation(o_raw[:, :], o_acc[:, :], ACT.Copy).then_inc(o_copied, 1)

            def evacuate(bank, u, dst, n_c, scale, bias):
                for c in range(n_c):
                    for n in range(NH):
                        act.wait_ge(work_full, 2 * bank + u + 1)
                        if scale is None:
                            a = act.activation(dst[:, c, tokens(n)], work[u % 2][:, :], ACT.Copy)
                        else:
                            a = act.activation(dst[:, c, tokens(n)], work[u % 2][:, :], ACT.Identity,
                                               scale=affine[:, scale, c:c + 1],
                                               bias=0.0 if bias is None else affine[:, bias, c:c + 1])
                        a.then_inc(work_free[u % 2], 1)
                        u += 1
                return u

            act.wait_ge(consts_in, 16 * 7)
            with act.Fori(0, B) as b:
                start = b * (BATCH_UNITS // 2)
                u = evacuate(start, 0, cT, CC, None, None)
                evacuate(start, u, hT, XC, 0, 1)
                run_layer(act, b, 0, unit, one_turn)
                evacuate(layer_start(b, 1) - MID_UNITS // 2, 0, hT, XC, 2, None)
                run_layer(act, b, 1, unit, one_turn, highs)

        @block.vector
        def _(dve):
            def unit(kind, i, bank, u, who):
                w = work[u % 2]
                full = 2 * bank + u + 1
                if kind in ("k", "q") and who.layer == 0:
                    dve.wait_ge(work_full, full)
                    dve.wait_ge(high_ok, 4 * who.sides + 2 * (kind == "q") + i + 1)
                    for h in range(G0):
                        hi = (k_parts if kind == "k" else q_high)[who.par][h][0:D0, tokens(i)].bitcast(F32)
                        lo = k_parts[who.par][h][D0:P, tokens(i)] if kind == "k" else q_low[who.par][h][0:D0, tokens(i)]
                        v = dve.tensor_tensor(lo, w[h * D0:(h + 1) * D0, :], hi, ALU.subtract)
                    v.then_inc(work_free[u % 2], 1)
                elif kind == "rowmax":
                    h, qt, n = i // (TT * NH), i // NH % TT, i % NH
                    dve.wait_ge(work_full, full)
                    dve.tensor_reduce(tile_max[:, h, qt, n:n + 1], w[:, :], AX.X, ALU.max, negate=True).then_inc(work_free[u % 2], 1)
                    if i % (TT * NH) == TT * NH - 1:
                        for k in range(2):
                            wait_unit_evacuated(dve, bank, u - k)
                        dve.tensor_reduce(neg_max[:, h, :], tile_max[:, h, :, :], AX.X, ALU.min).then_inc(neg_max_ok, 1)
                elif kind == "out":
                    if i == 0:
                        dve.wait_ge(recip_in, 16 * G1 * who.turns)
                        dve.wait_ge(o_copied, PRIMED + who.turns)
                        dve.tensor_tensor(o_norm[:, :], o_raw[:, :], recip[:, :], ALU.mult).then_inc(o_norm_ok, 1)
                        dve.wait_ge(bias_ok, who.b + 1)
                    dve.wait_ge(work_full, full)
                    dve.tensor_tensor(resid[:, i, :], w[:, :], resid[:, i, :], ALU.add).then_inc(work_free[u % 2], 1)

            def behind(kt, who):
                if kt == RECIP_AT:
                    g = (G0, G1)[who.layer]
                    dve.wait_ge(den_in, 16 * who.turns)
                    dve.reciprocal(recip_t[:, 0:g, :], den_t[:, 0:g, :]).then_inc(recip_ok, 1)

            def norms(kt, who, *_):
                n = NORM_STEPS * who.sides
                for which, at in ((0, 1), (1, 2)):
                    if kt == at:
                        m = n + 3 * which
                        vec = raw[which][:, :, :, :].rearrange("p t h d -> p (t h) d")
                        dve.wait_ge(rope_step, ROPE_STEPS * who.sides + 4 * (which + 1))
                        if which == 1:
                            dve.wait_ge(norm_step, n + 2)
                        dve.tensor_tensor(squares[:, :, :], vec, vec, ALU.mult).then_inc(norm_step, 1)
                        dve.wait_ge(norm_step, m + 1)
                        dve.tensor_reduce(sumsq[:, which, :], squares[:, :, :], AX.X, ALU.add).then_inc(norm_step, 1)
                        dve.wait_ge(norm_step, m + 2)
                        dve.tensor_scalar(sumsq[:, which, :], sumsq[:, which, :], L2_EPS ** 2, QK_SCALE ** -2, ALU.max, ALU.mult).then_inc(norm_step, 1)
                for which, at in ((0, 4), (1, 5)):
                    if kt == at:
                        m = n + 6 + 3 * which
                        dve.wait_ge(high1_ok, 2 * who.sides + which + 1)
                        vec = raw[which][:, :, :, :].rearrange("p t h d -> p (t h) d")
                        low = (2, 1)[which]
                        dve.tensor_tensor(stack[which][:, :, low, :], vec, stack[which][:, :, 0, :], ALU.subtract).then_inc(norm_step, 1)
                        dve.tensor_copy(stack[which][:, :, (1, 2)[which], :], stack[which][:, :, 0, :]).then_inc(norm_step, 1)
                        dve.wait_ge(norm_step, m + 1)
                        dve.tensor_copy(stack[which][:, :, 3, :], stack[which][:, :, low, :]).then_inc(norm_step, 1)

            def one_turn(l, b, p, par, j=None):
                t = Counts(b, l, p)
                who = shares(b, l, p, par, j)
                nxt, ahead, post = has(l, p, j)
                g = (G0, G1)[l]
                u = 0
                for kt in range(KT):
                    units = chunk(l, kt, nxt, ahead, post)
                    if post:
                        behind(kt, who["post"])
                        if kt == 1:
                            dve.wait_ge(work_full, 2 * t.bank + first_den(l, nxt) + NH)
                    for h in range(g):
                        s = kt * g + h
                        if kt > 0:
                            dve.wait_ge(exp_ok, t.steps + s + 1)
                            if kt > 1:
                                dve.wait_ge(add_ok, t.adds + (kt - 2) * g + h + 1)
                            before = probs[:, s - g, :] if kt == 1 else acc[h][:, :]
                            dve.tensor_tensor(acc[h][:, :], before, probs[:, s % RING, :], ALU.add).then_inc(add_ok, 1)
                        for kind, i, w in share(units, h, g):
                            unit(kind, i, t.bank, u, who[w])
                            u += 1
                    if l == 1 and nxt:
                        norms(kt, who["next"])

            def row_norm(l, b):
                n = 2 * b + l
                for t in range(TT):
                    v = dve.bn_stats(stats[:, t, :], resid[:, t, :])
                v.then_inc(bn_ok, 1)
                dve.wait_ge(bn_ok, n + 1)
                dve.memset(gate_v[:, 0:1], 0.0)
                for t in range(TT):
                    v = dve.bn_aggr(mv[:, t, :], stats[:, t, :])
                v.then_inc(aggr_ok, 1)
                dve.wait_ge(aggr_ok, n + 1)
                if l == 0:
                    dve.tensor_scalar(var_eps[:, :], mv[:, :, 1], LN_EPS, None, ALU.add).then_inc(var_ok, 1)
                else:
                    dve.tensor_tensor(mean_sq[:, :], mv[:, :, 0], mv[:, :, 0], ALU.mult).then_inc(mean_sq_step, 1)
                    dve.wait_ge(mean_sq_step, 2 * b + 1)
                    dve.tensor_tensor(mean_sq[:, :], mean_sq[:, :], mv[:, :, 1], ALU.add).then_inc(mean_sq_step, 1)
                    dve.wait_ge(mean_sq_step, 2 * b + 2)
                    dve.tensor_scalar(var_eps[:, :], mean_sq[:, :], RMS_EPS, None, ALU.add).then_inc(var_ok, 1)
                dve.wait_ge(rstd_ok, 2 * b + l + 1)
                for t in range(TT):
                    if l == 0:
                        v = dve.tensor_scalar(xn[:, t, :], resid[:, t, :], mv[:, t, 0:1], rstd[:, t:t + 1], ALU.subtract, ALU.mult)
                    else:
                        v = dve.tensor_scalar(xn[:, t, :], resid[:, t, :], rstd[:, t:t + 1], None, ALU.mult)
                    v.then_inc(xn_ok, 1)

            for n, counter in enumerate((work_free[0], work_free[1], o_copied, o_norm_ok)):
                dve.memset(gate_v[:, 1 + n:2 + n], 0.0).then_inc(counter, PRIMED)
            dve.memset(gate_v[:, 5:6], 0.0).then_inc(stored, 16 * PRIMED)
            dve.memset(ones[0][:, :], float(D0) ** 0.5)
            dve.memset(ones[1][:, :], 1.0)
            dve.wait_ge(consts_in, 16 * 7)
            dve.tensor_copy(ident_r[:, :], ident[:, :])
            dve.tensor_copy(ident_h[:, :], ident[:, :]).then_inc(consts_ok, 1)
            with dve.Fori(0, B) as b:
                dve.wait_ge(x_in, 16 * (b + 1))
                for i in range(2):
                    for h in range(G0):
                        dve.memset(k_one[i][h][D0:D0 + 1, :].bitcast(F32), 1.0)
                row_norm(0, b)
                run_layer(dve, b, 0, unit, one_turn, None, behind)
                wait_all_evacuated(dve, layer_start(b, 1) - MID_UNITS // 2)
                row_norm(1, b)
                run_layer(dve, b, 1, unit, one_turn, norms, behind)

        @block.gpsimd
        def _(pool):
            def unit(kind, i, bank, u, who):
                if kind == "k" and who.layer == 0:
                    pool.wait_ge(high_ok, 4 * who.sides + i + 1)
                    pool.tensor_tensor(gate_p[:, who.par * NH + i:who.par * NH + i + 1], power[:, 0:1], power[:, 0:1], ALU.mult)
                    for h in range(G0):
                        c = pool.tensor_copy(k_one[who.par][h][0:D0, tokens(i)], k_parts[who.par][h][0:D0, tokens(i)].bitcast(F32))
                    c.then_inc(dup_ok, 1)

            def rope(which, who):
                n = ROPE_STEPS * who.sides + 4 * which
                r, half = raw[which], D1 // 2
                c4 = cos[:, :, :].unsqueeze(2).broadcast_to([P, TT, G1, D1])
                s4 = sin[:, :, :].unsqueeze(2).broadcast_to([P, TT, G1, D1])
                if which == 1:
                    pool.wait_ge(rope_step, n)
                pool.tensor_tensor(rot[:, :, :, :], r[:, :, :, :], c4, ALU.mult).then_inc(rope_step, 1)
                pool.tensor_tensor(tmp[:, :, :, 0:half], r[:, :, :, half:D1], s4[:, :, :, 0:half], ALU.mult).then_inc(rope_step, 1)
                pool.tensor_tensor(tmp[:, :, :, half:D1], r[:, :, :, 0:half], s4[:, :, :, half:D1], ALU.mult).then_inc(rope_step, 1)
                pool.wait_ge(rope_step, n + 3)
                pool.tensor_tensor(r[:, :, :, :], rot[:, :, :, :], tmp[:, :, :, :], ALU.add).then_inc(rope_step, 1)

            def scale(which, who):
                n = ROPE_STEPS * who.sides + 8 + 2 * which
                vec = raw[which][:, :, :, :].rearrange("p t h d -> p (t h) d")
                pool.wait_ge(norm_step, NORM_STEPS * who.sides + 3 * (which + 1))
                pool.tensor_tensor(inv[:, which, :], sumsq[:, which, :], power[:, :], ALU.pow).then_inc(rope_step, 1)
                pool.wait_ge(rope_step, n + 1)
                pool.tensor_tensor(vec, vec, inv[:, which, :].unsqueeze(2).broadcast_to([P, TT * G1, D1]), ALU.mult).then_inc(rope_step, 1)

            def rotations(step, who, bank, evacuated):
                if step == 0:
                    wait_all_evacuated(pool, bank + evacuated // 2)
                    rope(0, who)
                    rope(1, who)
                    scale(0, who)
                    scale(1, who)

            def one_turn(l, b, p, par, j=None):
                t = Counts(b, l, p)
                who = shares(b, l, p, par, j)
                nxt, ahead, post = has(l, p, j)
                u = 0
                if l == 1 and nxt:
                    rotations(0, who["next"], t.bank, 0)
                for kt in range(KT):
                    for kind, i, w in chunk(l, kt, nxt, ahead, post):
                        unit(kind, i, t.bank, u, who[w])
                        u += 1

            def row_power(n):
                pool.wait_ge(var_ok, n + 1)
                pool.tensor_tensor(rstd[:, :], var_eps[:, :], power[:, 0:TT], ALU.pow).then_inc(rstd_ok, 1)

            pool.memset(power[:, :], -0.5).then_inc(power_ok, 1)
            pool.wait_ge(power_ok, 1)
            pool.wait_ge(consts_in, 16 * 7)
            with pool.Fori(0, B) as b:
                row_power(2 * b)
                pool.wait_ge(xn_ok, 2 * TT * b + TT)
                pool.tensor_tensor(resid[:, :, :], resid[:, :, :], bo_all[:, :].unsqueeze(1).broadcast_to([P, TT, D]), ALU.add).then_inc(bias_ok, 1)
                run_layer(pool, b, 0, unit, one_turn)
                row_power(2 * b + 1)
                run_layer(pool, b, 1, unit, one_turn, rotations)


_INS = ['x', 'ctx_768', 'L0_xattn_Wq', 'L0_xattn_Wk', 'L0_xattn_Wv', 'L0_xattn_Wo', 'L0_xattn_bo', 'L0_xattn_gamma',
        'L0_xattn_beta', 'L1_xattn_norm_w', 'L1_xattn_wq', 'L1_xattn_wkv', 'L1_xattn_wout']
_OUTS = [((B, S, D), 'float32')]


def rope_tables():
    inv_freq = 1.0 / 10000.0 ** (np.arange(0, D1, 2, dtype=np.float32) / D1)
    freqs = np.einsum('i,j->ij', np.arange(S, dtype=np.float32), inv_freq)
    emb = np.concatenate([freqs, freqs], axis=-1)
    sign = np.where(np.arange(D1) < D1 // 2, -1.0, 1.0)
    return np.cos(emb).astype(np.float32), (np.sin(emb) * sign).astype(np.float32)


def kernel(**inputs):
    import numpy as _np
    import concourse.bacc as _bacc
    from concourse import mybir as _mybir
    from concourse.bass_utils import run_bass_kernel_spmd as _run

    nc = _bacc.Bacc("TRN2", target_bir_lowering=False, num_devices=1)
    arrays, args = {}, []
    given = {name: _np.ascontiguousarray(inputs[name]) for name in _INS}
    given["cos"], given["sin"] = rope_tables()
    given["ident"] = _np.eye(P, dtype=_np.float32)
    for name, a in given.items():
        arrays[f"in_{name}_dram"] = a
        args.append(nc.dram_tensor(f"in_{name}_dram", a.shape, _mybir.dt.from_np(a.dtype), kind="ExternalInput").ap())
    for i, (shape, dtype) in enumerate(_OUTS):
        dt = _mybir.dt.from_np(_np.dtype(dtype))
        args.append(nc.dram_tensor(f"out_{i}_dram", shape, dt, kind="ExternalOutput").ap())
    rows = nc.dram_tensor("rows_dram", (2, G1, S), _mybir.dt.float32, kind="Internal").ap()
    build(nc, rows, *args)
    r = _run(nc, [arrays], core_ids=[0])
    got = tuple(r.results[0][f"out_{i}_dram"] for i in range(len(_OUTS)))
    return got[0]
```
